# Optimizing a Trainium2 kernel written in Bass

```python
import numpy as np
import jax
import jax.numpy as jnp

def _softmax(x, axis=-1):
    return jax.nn.softmax(x, axis=axis)

def _gelu(x):
    return jax.nn.gelu(x, approximate=True)

def _silu(x):
    return jax.nn.silu(x)

def _sigmoid(x):
    return jax.nn.sigmoid(x)

def _layernorm(x, axis=-1, eps=1e-05):
    m = jnp.mean(x, axis=axis, keepdims=True)
    v = jnp.var(x, axis=axis, keepdims=True)
    return (x - m) / jnp.sqrt(v + eps)

def _scatter_add(tgt, idx, src, axis=0):
    return tgt.at[idx].add(src)

def _segment_sum(src, seg, n):
    return jax.ops.segment_sum(src, seg, n)
kernel_name = 'mk_flamingo_gated_d1_seqx_r4_0e9701'

def setup_inputs(seed: int=0):
    np.random.seed(seed)
    _w = jnp.asarray

    def _rec_inputs():
        import jax
        import jax.numpy as jnp
        _rk = jax.random.key(seed)
        x = -0.0003929 + 0.9999 * jax.random.normal(jax.random.fold_in(_rk, 1), (8, 256, 256), jnp.float32)
        _lenS = 256 - jax.random.randint(jax.random.fold_in(_rk, 7), (8,), 0, max(1, 256 // 4) + 1, jnp.int32)
        _lenS2 = 256 - jax.random.randint(jax.random.fold_in(_rk, 8), (8,), 0, max(1, 256 // 4) + 1, jnp.int32)
        _ctx_1024P = jax.random.normal(jax.random.fold_in(_rk, 11), (8, 16, 256), jnp.float32)
        _ctx_1024c = jax.random.dirichlet(jax.random.fold_in(_rk, 511), 0.3 * jnp.ones((16,), jnp.float32), (8, 256))
        _ctx_1024t = jnp.einsum('bsk,bkd->bsd', _ctx_1024c, _ctx_1024P)
        _ctx_1024t = _ctx_1024t * jax.lax.rsqrt(jnp.mean(jnp.square(_ctx_1024t)) + 1e-12) * 0.953939
        ctx_1024 = 2.81802e-05 + 1.00001 * (_ctx_1024t + 0.3 * jax.random.normal(jax.random.fold_in(_rk, 611), (8, 256, 256), jnp.float32))
        _validS = jnp.arange(256)[None, :] < _lenS[:, None]
        _validS2 = jnp.arange(256)[None, :] < _lenS2[:, None]
        _causal = jnp.tril(jnp.ones((256, 256), dtype=bool))
        mask_BxSxS2_ik1 = jnp.where(jnp.broadcast_to(_validS2[:, None, :], (8, 256, 256)), 1, 0).astype(jnp.int32)
        _g = jax.random.normal(jax.random.fold_in(_rk, 9001), (2, 1), jnp.float32)
        _g = jnp.sign(_g) * jnp.maximum(jnp.abs(_g), 1.0) + (_g == 0) * 1.0
        g_xattn = _g[0]
        g_ffn = _g[1]
        return (x, ctx_1024, mask_BxSxS2_ik1, g_xattn, g_ffn)
    x, ctx_1024, mask_BxSxS2_ik1, g_xattn, g_ffn = _rec_inputs()

    def _L0_xattn_setup():
        import jax, jax.numpy as jnp
        import numpy as np
        B, L, H = (8, 512, 256)
        SCALE = float(np.sqrt(H))
        EPS = 1e-05
        key = jax.random.key(seed)
        ks = jax.random.split(key, 12)
        s = 1.0 / np.sqrt(H)
        return {'queries': jax.random.normal(ks[0], (B, L, H), jnp.float32), 'keys': jax.random.normal(ks[1], (B, L, H), jnp.float32), 'values': jax.random.normal(ks[2], (B, L, H), jnp.float32), 'mask': jax.random.randint(ks[3], (B, L, L), 0, 2, jnp.int32), 'Wq': jax.random.normal(ks[4], (H, H), jnp.float32) * s, 'bq': jnp.zeros((H,), jnp.float32), 'Wk': jax.random.normal(ks[5], (H, H), jnp.float32) * s, 'bk': jnp.zeros((H,), jnp.float32), 'Wv': jax.random.normal(ks[6], (H, H), jnp.float32) * s, 'bv': jnp.zeros((H,), jnp.float32), 'ln_gamma': jnp.ones((H,), jnp.float32), 'ln_beta': jnp.zeros((H,), jnp.float32)}
    _L0_xattn_all = _L0_xattn_setup()
    _L0_xattn_in = {k: v for k, v in _L0_xattn_all.items() if k in ('Wq', 'bq', 'Wk', 'bk', 'Wv', 'bv', 'ln_gamma', 'ln_beta')}
    del _L0_xattn_all

    def _L0_ffn_setup():
        import jax, jax.numpy as jnp
        import numpy as np
        DIM = 256
        DEPTH = 2
        HEADS = 8
        DIM_HEAD = 64
        WINDOW = 128
        INNER = HEADS * DIM_HEAD
        HID = int(DIM * 4 * 2 / 3)
        B, N = (2, 2048)
        QK_SCALE = 8.0

        def shift_token(t):
            t1, t2 = jnp.split(t, 2, axis=-1)
            t2 = jnp.pad(t2, ((0, 0), (1, 0), (0, 0)))[:, :-1]
            return jnp.concatenate([t1, t2], axis=-1)

        def l2norm(t):
            return t / jnp.clip(jnp.linalg.norm(t, axis=-1, keepdims=True), 1e-12)

        def rotate_half(x):
            x1, x2 = jnp.split(x, 2, axis=-1)
            return jnp.concatenate([-x2, x1], axis=-1)

        def rotary_xpos(q, k):
            n = q.shape[-2]
            half_idx = jnp.arange(0, DIM_HEAD, 2, dtype=jnp.float32)
            inv_freq = 1.0 / 10000.0 ** (half_idx / DIM_HEAD)
            t = jnp.arange(n, dtype=jnp.float32)
            freqs = t[:, None] * inv_freq[None, :]
            freqs = jnp.concatenate([freqs, freqs], axis=-1)
            base = (half_idx + 0.4 * DIM_HEAD) / (1.4 * DIM_HEAD)
            power = (t - n // 2) / float(WINDOW // 2)
            scale = base[None, :] ** power[:, None]
            scale = jnp.concatenate([scale, scale], axis=-1)
            cos, sin = (jnp.cos(freqs), jnp.sin(freqs))
            q = q * cos * scale + rotate_half(q) * sin * scale
            k = k * cos / scale + rotate_half(k) * sin / scale
            return (q, k)

        def local_attention(q, k, v):
            b, h, n, d = q.shape
            w = n // WINDOW
            bq = q.reshape(b, h, w, WINDOW, d) * QK_SCALE
            bk = k.reshape(b, h, w, WINDOW, d)
            bv = v.reshape(b, h, w, WINDOW, d)

            def look_around(t):
                p = jnp.pad(t, ((0, 0), (0, 0), (1, 0), (0, 0), (0, 0)))
                return jnp.concatenate([p[:, :, :w], p[:, :, 1:]], axis=3)
            bk, bv = (look_around(bk), look_around(bv))
            bt = jnp.arange(n).reshape(w, WINDOW)
            btp = jnp.pad(bt, ((1, 0), (0, 0)), constant_values=-1)
            btk = jnp.concatenate([btp[:w], btp[1:]], axis=1)
            sim = jnp.einsum('bhwid,bhwjd->bhwij', bq, bk)
            i = bt[:, :, None]
            j = btk[:, None, :]
            mask = (i < j) | (i > j + WINDOW) | (j == -1)
            sim = jnp.where(mask, -jnp.finfo(sim.dtype).max, sim)
            attn = jax.nn.softmax(sim, axis=-1)
            out = jnp.einsum('bhwij,bhwjd->bhwid', attn, bv)
            return out.reshape(b, h, n, d)

        def _layer(x, wqkv, qs, ksc, wo, lg, lb, w1, b1, w2, b2):
            b, n, _ = x.shape
            h = shift_token(x)
            qkv = h @ wqkv
            q, k, v = jnp.split(qkv, 3, axis=-1)
            to_heads = lambda t: t.reshape(b, n, HEADS, DIM_HEAD).transpose(0, 2, 1, 3)
            q, k, v = (to_heads(q), to_heads(k), to_heads(v))
            q = l2norm(q) * qs
            k = l2norm(k) * ksc
            q, k = rotary_xpos(q, k)
            o = local_attention(q, k, v)
            o = o.transpose(0, 2, 1, 3).reshape(b, n, INNER)
            x = x + o @ wo
            h = shift_token(x)
            mu = h.mean(-1, keepdims=True)
            var = h.var(-1, keepdims=True)
            h = (h - mu) / jnp.sqrt(var + 1e-05) * lg + lb
            h = h @ w1 + b1
            a, g = jnp.split(h, 2, axis=-1)
            h = a * jax.nn.gelu(g, approximate=False)
            x = x + h @ w2 + b2
            return x
        key = jax.random.key(seed)
        ks = jax.random.split(key, 6)
        return {'x': jax.random.normal(ks[0], (B, N, DIM), jnp.float32), 'wqkv': jax.random.normal(ks[1], (DEPTH, DIM, 3 * INNER), jnp.float32) * 0.02, 'q_scale': jnp.ones((DEPTH, DIM_HEAD), jnp.float32), 'k_scale': jnp.ones((DEPTH, DIM_HEAD), jnp.float32), 'wo': jax.random.normal(ks[2], (DEPTH, INNER, DIM), jnp.float32) * 0.02, 'ln_g': jnp.ones((DEPTH, DIM), jnp.float32), 'ln_b': jnp.zeros((DEPTH, DIM), jnp.float32), 'w1': jax.random.normal(ks[3], (DEPTH, DIM, 2 * HID), jnp.float32) * 0.02, 'b1': jnp.zeros((DEPTH, 2 * HID), jnp.float32), 'w2': jax.random.normal(ks[4], (DEPTH, HID, DIM), jnp.float32) * 0.02, 'b2': jnp.zeros((DEPTH, DIM), jnp.float32)}
    _L0_ffn_all = _L0_ffn_setup()
    _L0_ffn_in = {k: v for k, v in _L0_ffn_all.items() if k in ('wqkv', 'q_scale', 'k_scale', 'wo', 'ln_g', 'ln_b', 'w1', 'b1', 'w2', 'b2')}
    del _L0_ffn_all
    return {'x': x, 'ctx_1024': ctx_1024, 'mask_BxSxS2_ik1': mask_BxSxS2_ik1, 'g_xattn': g_xattn, 'g_ffn': g_ffn, 'L0_xattn_Wq': _L0_xattn_in['Wq'], 'L0_xattn_bq': _L0_xattn_in['bq'], 'L0_xattn_Wk': _L0_xattn_in['Wk'], 'L0_xattn_bk': _L0_xattn_in['bk'], 'L0_xattn_Wv': _L0_xattn_in['Wv'], 'L0_xattn_bv': _L0_xattn_in['bv'], 'L0_xattn_ln_gamma': _L0_xattn_in['ln_gamma'], 'L0_xattn_ln_beta': _L0_xattn_in['ln_beta'], 'L0_ffn_wqkv': _L0_ffn_in['wqkv'], 'L0_ffn_q_scale': _L0_ffn_in['q_scale'], 'L0_ffn_k_scale': _L0_ffn_in['k_scale'], 'L0_ffn_wo': _L0_ffn_in['wo'], 'L0_ffn_ln_g': _L0_ffn_in['ln_g'], 'L0_ffn_ln_b': _L0_ffn_in['ln_b'], 'L0_ffn_w1': _L0_ffn_in['w1'], 'L0_ffn_b1': _L0_ffn_in['b1'], 'L0_ffn_w2': _L0_ffn_in['w2'], 'L0_ffn_b2': _L0_ffn_in['b2']}

def reference(x, ctx_1024, mask_BxSxS2_ik1, g_xattn, g_ffn, L0_xattn_Wq, L0_xattn_bq, L0_xattn_Wk, L0_xattn_bk, L0_xattn_Wv, L0_xattn_bv, L0_xattn_ln_gamma, L0_xattn_ln_beta, L0_ffn_wqkv, L0_ffn_q_scale, L0_ffn_k_scale, L0_ffn_wo, L0_ffn_ln_g, L0_ffn_ln_b, L0_ffn_w1, L0_ffn_b1, L0_ffn_w2, L0_ffn_b2):
    import jax
    import jax.numpy as jnp

    def _L0_xattn_ref(queries, keys, values, mask, Wq, bq, Wk, bk, Wv, bv, ln_gamma, ln_beta):
        import jax, jax.numpy as jnp
        import numpy as np
        B, L, H = (8, 512, 256)
        SCALE = float(np.sqrt(H))
        EPS = 1e-05
        Q = queries @ Wq + bq
        K = keys @ Wk + bk
        V = values @ Wv + bv
        scores = jnp.einsum('bik,bjk->bij', Q, K) / SCALE
        scores = jnp.where(mask == 0, -jnp.inf, scores)
        probs = jax.nn.softmax(scores, axis=-1)
        context = jnp.einsum('bij,bjk->bik', probs, V)
        mu = jnp.mean(context, axis=-1, keepdims=True)
        var = jnp.var(context, axis=-1, keepdims=True)
        normed = (context - mu) * jax.lax.rsqrt(var + EPS)
        return normed * ln_gamma + ln_beta

    def _L0_ffn_ref(x, wqkv, q_scale, k_scale, wo, ln_g, ln_b, w1, b1, w2, b2):
        import jax, jax.numpy as jnp
        import numpy as np
        DIM = 256
        DEPTH = 2
        HEADS = 8
        DIM_HEAD = 64
        WINDOW = 128
        INNER = HEADS * DIM_HEAD
        HID = int(DIM * 4 * 2 / 3)
        B, N = (2, 2048)
        QK_SCALE = 8.0

        def shift_token(t):
            t1, t2 = jnp.split(t, 2, axis=-1)
            t2 = jnp.pad(t2, ((0, 0), (1, 0), (0, 0)))[:, :-1]
            return jnp.concatenate([t1, t2], axis=-1)

        def l2norm(t):
            return t / jnp.clip(jnp.linalg.norm(t, axis=-1, keepdims=True), 1e-12)

        def rotate_half(x):
            x1, x2 = jnp.split(x, 2, axis=-1)
            return jnp.concatenate([-x2, x1], axis=-1)

        def rotary_xpos(q, k):
            n = q.shape[-2]
            half_idx = jnp.arange(0, DIM_HEAD, 2, dtype=jnp.float32)
            inv_freq = 1.0 / 10000.0 ** (half_idx / DIM_HEAD)
            t = jnp.arange(n, dtype=jnp.float32)
            freqs = t[:, None] * inv_freq[None, :]
            freqs = jnp.concatenate([freqs, freqs], axis=-1)
            base = (half_idx + 0.4 * DIM_HEAD) / (1.4 * DIM_HEAD)
            power = (t - n // 2) / float(WINDOW // 2)
            scale = base[None, :] ** power[:, None]
            scale = jnp.concatenate([scale, scale], axis=-1)
            cos, sin = (jnp.cos(freqs), jnp.sin(freqs))
            q = q * cos * scale + rotate_half(q) * sin * scale
            k = k * cos / scale + rotate_half(k) * sin / scale
            return (q, k)

        def local_attention(q, k, v):
            b, h, n, d = q.shape
            w = n // WINDOW
            bq = q.reshape(b, h, w, WINDOW, d) * QK_SCALE
            bk = k.reshape(b, h, w, WINDOW, d)
            bv = v.reshape(b, h, w, WINDOW, d)

            def look_around(t):
                p = jnp.pad(t, ((0, 0), (0, 0), (1, 0), (0, 0), (0, 0)))
                return jnp.concatenate([p[:, :, :w], p[:, :, 1:]], axis=3)
            bk, bv = (look_around(bk), look_around(bv))
            bt = jnp.arange(n).reshape(w, WINDOW)
            btp = jnp.pad(bt, ((1, 0), (0, 0)), constant_values=-1)
            btk = jnp.concatenate([btp[:w], btp[1:]], axis=1)
            sim = jnp.einsum('bhwid,bhwjd->bhwij', bq, bk)
            i = bt[:, :, None]
            j = btk[:, None, :]
            mask = (i < j) | (i > j + WINDOW) | (j == -1)
            sim = jnp.where(mask, -jnp.finfo(sim.dtype).max, sim)
            attn = jax.nn.softmax(sim, axis=-1)
            out = jnp.einsum('bhwij,bhwjd->bhwid', attn, bv)
            return out.reshape(b, h, n, d)

        def _layer(x, wqkv, qs, ksc, wo, lg, lb, w1, b1, w2, b2):
            b, n, _ = x.shape
            h = shift_token(x)
            qkv = h @ wqkv
            q, k, v = jnp.split(qkv, 3, axis=-1)
            to_heads = lambda t: t.reshape(b, n, HEADS, DIM_HEAD).transpose(0, 2, 1, 3)
            q, k, v = (to_heads(q), to_heads(k), to_heads(v))
            q = l2norm(q) * qs
            k = l2norm(k) * ksc
            q, k = rotary_xpos(q, k)
            o = local_attention(q, k, v)
            o = o.transpose(0, 2, 1, 3).reshape(b, n, INNER)
            x = x + o @ wo
            h = shift_token(x)
            mu = h.mean(-1, keepdims=True)
            var = h.var(-1, keepdims=True)
            h = (h - mu) / jnp.sqrt(var + 1e-05) * lg + lb
            h = h @ w1 + b1
            a, g = jnp.split(h, 2, axis=-1)
            h = a * jax.nn.gelu(g, approximate=False)
            x = x + h @ w2 + b2
            return x
        for l in range(DEPTH):
            x = _layer(x, wqkv[l], q_scale[l], k_scale[l], wo[l], ln_g[l], ln_b[l], w1[l], b1[l], w2[l], b2[l])
        return x
    x = x + jnp.tanh(g_xattn[0]) * _L0_xattn_ref(_layernorm(x, axis=-1), ctx_1024, ctx_1024, mask_BxSxS2_ik1, L0_xattn_Wq, L0_xattn_bq, L0_xattn_Wk, L0_xattn_bk, L0_xattn_Wv, L0_xattn_bv, L0_xattn_ln_gamma, L0_xattn_ln_beta)
    x = x + jnp.tanh(g_ffn[0]) * _L0_ffn_ref(_layernorm(x, axis=-1), L0_ffn_wqkv, L0_ffn_q_scale, L0_ffn_k_scale, L0_ffn_wo, L0_ffn_ln_g, L0_ffn_ln_b, L0_ffn_w1, L0_ffn_b1, L0_ffn_w2, L0_ffn_b2)
    return x

_drawn_inputs = setup_inputs


def setup_inputs(seed=0):
    import zlib

    import numpy as np

    out = dict(_drawn_inputs(seed))
    spreads = {'L0_xattn_bq': (0.0, 0.34),
     'L0_xattn_bk': (0.0, 0.8),
     'L0_xattn_bv': (0.0, 0.1),
     'L0_xattn_ln_gamma': (1.0, 0.2),
     'L0_xattn_ln_beta': (0.0, 0.1),
     'L0_ffn_q_scale': (1.0, 0.6),
     'L0_ffn_k_scale': (1.0, 0.6),
     'L0_ffn_ln_g': (1.0, 0.2),
     'L0_ffn_ln_b': (0.0, 0.513),
     'L0_ffn_b1': (0.0, 0.1),
     'L0_ffn_b2': (0.0, 0.1)}
    factors = {}
    for name, (base, spread) in spreads.items():
        noise = np.random.default_rng([zlib.crc32(name.encode()), seed]).standard_normal(out[name].shape)
        drawn = base * np.exp(spread * noise) if base else spread * noise
        out[name] = jnp.asarray(drawn.astype(out[name].dtype))
    for name, factor in factors.items():
        out[name] = (out[name] * factor).astype(out[name].dtype)
    return out
```

```python
from contextlib import ExitStack

import concourse.bass as bass
from concourse import mybir

P = 128
F32 = mybir.dt.float32
I32 = mybir.dt.int32
ALU = mybir.AluOpType
ACT = mybir.ActivationFunctionType
AX = mybir.AxisListType

NEG = -1.0e30
LN_EPS = 1e-5
L2_EPS2 = 1e-24
HEADS, DH = 8, 64
QK_SCALE = 8.0
FMAX_DMA = 16


def wait(eng, semaphore, value):
    if isinstance(value, int) and value <= 0:
        return
    eng.wait_ge(semaphore, value)


def wait_apart(eng, passed, *waits):
    for semaphore, value in waits:
        wait(eng, semaphore, value)
    eng.sem_inc(passed, 1)


def build(nc, x, ctx_in, mask, g_xattn, g_ffn, Wq, bq, Wk, bk, Wv, bv, ln_gamma, ln_beta,
          wqkv, q_scale, k_scale, wo, ln_g, ln_b, w1, b1, w2, b2, rot_tab, win_mask, ident_in, out):
    NB, S, D = x.shape
    T = S // P
    KC = D // P
    DEPTH = wqkv.shape[0]
    INNER = HEADS * DH
    PAIRS = HEADS // 2
    HID = w2.shape[1]
    HC = (HID + P - 1) // P
    HT = HID - (HC - 1) * P
    hrows = [P] * (HC - 1) + [HT]
    STEPS = DEPTH * NB
    XSCALE = float(D) ** -0.5
    YTC = S + 3
    NS = 3
    assert S == 2 * P and D == 2 * P and DEPTH == 2

    xmid = nc.dram_tensor("xmid", [NB, P, T * D], F32, kind="Internal").ap()
    ystream = nc.dram_tensor("ystream", [STEPS, P, T * D], F32, kind="Internal").ap()

    st = ExitStack()
    with st:
        def sb(name, shape, dt=F32):
            return st.enter_context(nc.sbuf_tensor(name, shape, dt))

        def sem(name):
            return st.enter_context(nc.semaphore(name))

        wq_sb, wk_sb, wv_sb = (sb(n, [P, KC, D]) for n in ("wq_sb", "wk_sb", "wv_sb"))
        wqkv_sb = [sb(f"wqkv_sb{l}", [P, KC, 3 * INNER]) for l in range(DEPTH)]
        wo_sb = [sb(f"wo_sb{l}", [P, PAIRS, D]) for l in range(DEPTH)]
        w1_sb = [sb(f"w1_sb{l}", [P, KC, 2 * HID]) for l in range(DEPTH)]
        w2_sb = [sb(f"w2_sb{l}", [P, HC, D]) for l in range(DEPTH)]
        ident = sb("ident", [P, P])
        wmask = sb("wmask", [P, 3 * P])
        rtab = sb("rtab", [P, T, 2, 2 * DH])
        qks = sb("qks", [P, DEPTH, 2 * DH])
        tc_sb = [sb(f"tc_sb{l}", [P, T, 2, DH]) for l in range(DEPTH)]
        ts_sb = [sb(f"ts_sb{l}", [P, T, 2, DH]) for l in range(DEPTH)]
        bqk = sb("bqk", [P, 2, KC])
        bv_bc = sb("bv_bc", [P, D])
        gam_bc = sb("gam_bc", [P, D])
        bet_bc = sb("bet_bc", [P, D])
        b2_bc = [sb(f"b2_bc{l}", [P, D]) for l in range(DEPTH)]
        lgb = sb("lgb", [P, DEPTH, 2, KC])
        b1_sb = sb("b1_sb", [P, DEPTH, 2, HC])
        g_in = sb("g_in", [P, 2])
        tg = sb("tg", [P, 2])
        nhalf = sb("nhalf", [P, 2 * HEADS])

        x_in = sb("x_in", [P, T, D])
        c_in = sb("c_in", [P, T, D])
        m_in = sb("m_in", [P, T, S], I32)
        x_res = sb("x_res", [P, T, D])
        xn = sb("xn", [P, T, D])
        xnT = sb("xnT", [P, KC, S])
        cT = sb("cT", [P, KC, S])
        xqT = sb("xqT", [P, KC, S])
        xkT = sb("xkT", [P, KC, S])
        xv = sb("xv", [P, T, D])
        mbias = sb("mbias", [P, T, S])
        xs = sb("xs", [P, T, S])
        xp = sb("xp", [P, T, S])
        xpT = sb("xpT", [P, T, S])
        xc = sb("xc", [P, T, D])
        x_mid = sb("x_mid", [P, T, D])
        y_new = sb("y_new", [P, T, D])
        xst = sb("xst", [P, T, 6])
        xmv = sb("xmv", [P, 3, T, 2])
        xrs = sb("xrs", [P, 3, T])
        xmx, xnb, xl, xrl = (sb(n, [P, T]) for n in ("xmx", "xnb", "xl", "xrl"))

        y_next = sb("y_next", [P, T, D])
        y_res = sb("y_res", [P, T, D])
        yT = sb("yT", [P, KC * YTC])
        t1 = sb("t1", [P, T, 2 * INNER])
        t2 = sb("t2", [P, T, 2 * INNER])
        sqb = sb("sqb", [P, 2 * INNER])
        ss = sb("ss", [P, T, 2 * HEADS])
        rn = sb("rn", [P, T, 2 * HEADS])
        rn8 = sb("rn8", [P, T, HEADS])
        nrn8 = sb("nrn8", [P, T, HEADS])
        qz = sb("qz", [P, HEADS, S])
        kT = sb("kT", [P, PAIRS, S])
        vz = sb("vz", [P, T, PAIRS, 3, DH])
        sm = sb("sm", [P, NS, 3 * P])
        pr = sb("pr", [P, NS, 3 * P])
        pT = sb("pT", [P, 2, 3 * P])
        mx, nb, ls, rl = (sb(n, [P, HEADS, T]) for n in ("mx", "nb", "ls", "rl"))
        oT = sb("oT", [P, PAIRS, S])
        x1 = sb("x1", [P, T, D])
        hb = sb("hb", [P, T, D])
        hst = sb("hst", [P, T, 6])
        hmv = sb("hmv", [P, T, 2])
        hrs = sb("hrs", [P, T])
        hn = sb("hn", [P, T, D])
        hT = sb("hT", [P, KC, S])
        gl = sb("gl", [P, 2, S])
        u = sb("u", [P, HC, S])
        x1b = sb("x1b", [P, T, D])
        yo = sb("yo", [P, T, D])
        xm_res = sb("xm_res", [P, T, D])

        ps = st.enter_context(nc.psum_tensor("ps", [P, 8, 512], F32))

        def bank(i):
            return ps[:, i, :]

        def halves(i):
            return ps[:, i, :].rearrange("p (t n) -> p t n", t=2)

        wx_in, w0_in, w1_in, cst_in, cst2_in = (
            sem(n) for n in ("wx_in", "w0_in", "w1_in", "cst_in", "cst2_in"))
        zeros_set, tanh_done, prep_done = sem("zeros_set"), sem("tanh_done"), sem("prep_done")
        dve_passed, pool_passed = sem("dve_passed"), sem("pool_passed")
        x_loaded, c_loaded, m_loaded, xres_loaded = (
            sem(n) for n in ("x_loaded", "c_loaded", "m_loaded", "xres_loaded"))
        xmid_stored, y_stored = sem("xmid_stored"), sem("y_stored")
        (xbn, xvar, xrstd_a, xrstd, xn_done, c_tr, xn_tr, cT_done, xnT_done, k_mm, q_mm, v_mm, kT_x, qT_x,
         v_x, s_mm, mb_done, smax, nbx, exp_x, rlx, p_tr, pT_x, ctx_mm, xc_done, tn_done, tg_done,
         xmid_done, xrb_done, y_done_x) = (sem(n) for n in (
             "xbn", "xvar", "xrstd_a", "xrstd", "xn_done", "c_tr", "xn_tr", "cT_done", "xnT_done", "k_mm", "q_mm",
             "v_mm", "kT_x", "qT_x", "v_x", "s_mm", "mb_done", "smax", "nbx", "exp_x", "rlx", "p_tr",
             "pT_x", "ctx_mm", "xc_done", "tn_done", "tg_done", "xmid_done", "xrb_done", "y_done_x"))
        ynext_in, yres_in, xm_in, h_in, res_stored = (
            sem(n) for n in ("ynext_in", "yres_in", "xm_in", "h_in", "res_stored"))
        (y_tr, yT_done, qk_mm, v_mm2, sq_done, ss_done, ssc_done, rn_done, rn8_done, rot_done, qs_done,
         ka_done, ks_done, v_done, qk_tr, q_done, k_done, s_mm2, mx_done, nb_done, e_done, rl_done,
         pn_done, pt_tr, pT_done, pv_mm, o_done, wo_mm, x1_done, hbn_a, hbn, heps, hrstd, hn_done, h_tr,
         hT_done, up_mm, gl_done, u_done, xb_done, dn_mm, yo_done, res_done) = (sem(n) for n in (
             "y_tr", "yT_done", "qk_mm", "v_mm2", "sq_done", "ss_done", "ssc_done", "rn_done", "rn8_done",
             "rot_done", "qs_done", "ka_done", "ks_done", "v_done", "qk_tr", "q_done", "k_done", "s_mm2",
             "mx_done", "nb_done", "e_done", "rl_done", "pn_done", "pt_tr", "pT_done", "pv_mm", "o_done",
             "wo_mm", "x1_done", "hbn_a", "hbn", "heps", "hrstd", "hn_done", "h_tr", "hT_done", "up_mm",
             "gl_done", "u_done", "xb_done", "dn_mm", "yo_done", "res_done"))

        block = st.enter_context(nc.Block())

        def rows(ap):
            return ap.rearrange("(t p) d -> p t d", p=P)

        def flat(t):
            return t[:].rearrange("p t d -> p (t d)")

        def run_x(eng, turn):
            turn(0, True, False)
            turn(1, True, True)
            with eng.Fori(2, NB) as b:
                turn(b, True, True)
            turn(NB, False, True)

        def run_steps(eng, step):
            step(0, 0, None)
            step(1, 0, 0)
            with eng.Fori(2, NB) as s:
                step(s, 0, 0)
            step(NB, 1, 0)
            with eng.Fori(NB + 1, STEPS - 1) as s:
                step(s, 1, 1)
            step(STEPS - 1, 1, 1)
            step(STEPS, None, 1)

        @block.sync
        def _(sp):
            n = 0
            for w, dst in ((Wk, wk_sb), (Wq, wq_sb), (Wv, wv_sb)):
                sp.dma_start(dst[:], w.rearrange("(k p) n -> p k n", p=P)).then_inc(wx_in, 16)
            small = [(ident[:], ident_in), (wmask[:], win_mask), (rtab[:], rot_tab),
                     (bqk[:, 0, :], bq.rearrange("(m p) -> p m", p=P)),
                     (bqk[:, 1, :], bk.rearrange("(m p) -> p m", p=P)),
                     (bv_bc[:], bv.partition_broadcast(P)),
                     (gam_bc[:], ln_gamma.partition_broadcast(P)),
                     (bet_bc[:], ln_beta.partition_broadcast(P)),
                     (g_in[:, 0:1], g_xattn.partition_broadcast(P)),
                     (g_in[:, 1:2], g_ffn.partition_broadcast(P))]
            for l in range(DEPTH):
                small += [(b2_bc[l][:], b2[l, :].partition_broadcast(P)),
                          (qks[:, l, 0:DH], q_scale[l, :].partition_broadcast(P)),
                          (qks[:, l, DH:2 * DH], k_scale[l, :].partition_broadcast(P)),
                          (lgb[:, l, 0, :], ln_g[l, :].rearrange("(k p) -> p k", p=P)),
                          (lgb[:, l, 1, :], ln_b[l, :].rearrange("(k p) -> p k", p=P))]
                for half in range(2):
                    o = half * HID
                    small += [(b1_sb[:, l, half, 0:HC - 1],
                               b1[l, o:o + HID - HT].rearrange("(c p) -> p c", p=P)),
                              (b1_sb[0:HT, l, half, HC - 1:HC],
                               b1[l, o + HID - HT:o + HID].unsqueeze(1))]
            assert 16 * len(small[10:]) == CONSTS
            for dst, src in small[:10]:
                sp.dma_start(dst, src, allow_slow_non_contiguous=True).then_inc(cst_in, 16)

            def load_layer(l, semaphore):
                sp.dma_start(wqkv_sb[l][:], wqkv[l].rearrange("(k p) n -> p k n", p=P)).then_inc(semaphore, 16)
                sp.dma_start(wo_sb[l][:], wo[l].rearrange("(k p) n -> p k n", p=P)).then_inc(semaphore, 16)
                sp.dma_start(w1_sb[l][:], w1[l].rearrange("(k p) n -> p k n", p=P)).then_inc(semaphore, 16)
                sp.dma_start(w2_sb[l][:, 0:HC - 1, :],
                             w2[l, 0:HID - HT, :].rearrange("(c p) n -> p c n", p=P)).then_inc(semaphore, 16)
                sp.dma_start(w2_sb[l][0:HT, HC - 1, :], w2[l, HID - HT:HID, :]).then_inc(semaphore, 16)

            def turn(b, project, finish):
                if project:
                    wait(sp, c_tr, b)
                    sp.dma_start(c_in[:], rows(ctx_in[b])).then_inc(c_loaded, 16)
                    wait(sp, xn_done, T * b)
                    sp.dma_start(x_in[:], rows(x[b])).then_inc(x_loaded, 16)
                    wait(sp, mb_done, b)
                    sp.dma_start(m_in[:], rows(mask[b])).then_inc(m_loaded, 16)
                if finish:
                    wait(sp, xmid_done, b - 1)
                    sp.dma_start(x_res[:], rows(x[b - 1])).then_inc(xres_loaded, 16)
                    sp.wait_ge(xmid_done, b)
                    sp.dma_start(xmid[b - 1], flat(x_mid)).then_inc(xmid_stored, 16)
                    sp.wait_ge(y_done_x, T * b)
                    sp.dma_start(ystream[b - 1], flat(y_new)).then_inc(y_stored, 16)
                if isinstance(b, int) and b == 0:
                    for dst, src in small[10:]:
                        sp.dma_start(dst, src, allow_slow_non_contiguous=True).then_inc(cst2_in, 16)
                    sp.wait_ge(zeros_set, ZEROS)
                    load_layer(0, w0_in)
                    load_layer(1, w1_in)

            run_x(sp, turn)

            sp.wait_ge(y_stored, 16)
            sp.dma_start(flat(y_next), ystream[0]).then_inc(ynext_in, 16)
            sp.wait_ge(y_stored, 16 * NB)
            sp.wait_ge(xmid_stored, 16 * NB)

            def step(s, la, lf):
                f = s - 1
                if la is not None:
                    wait(sp, x1_done, s)
                    sp.dma_start(flat(y_res), ystream[s]).then_inc(yres_in, 16)
                    if not (isinstance(s, int) and s == STEPS - 1):
                        wait(sp, y_tr, s + 1)
                        if la == 0:
                            wait(sp, res_stored, 16 * f)
                        else:
                            sp.wait_ge(res_stored, 16 * (s + 2 - NB))
                        sp.dma_start(flat(y_next), ystream[s + 1]).then_inc(ynext_in, 16)
                if lf == 1:
                    sp.wait_ge(res_done, f)
                    sp.dma_start(flat(xm_res), xmid[f - NB]).then_inc(xm_in, 16)
                if lf is not None:
                    sp.wait_ge(res_done, s)
                    sp.dma_start(rows(out[f - NB]) if lf else ystream[f + NB].rearrange("p (t d) -> p t d", t=T),
                                 yo[:]).then_inc(res_stored, 16)
                if la is not None:
                    sp.wait_ge(x1_done, s + 1)
                    wait(sp, hn_done, s)
                    sp.dma_start(hb[:, :, 0:P], x1[:, :, 0:P]).then_inc(h_in, 16)
                    a = P - 16
                    sp.dma_start(hb[1:a + 1, :, P:D], x1[0:a, :, P:D]).then_inc(h_in, 16)
                    sp.dma_start(hb[a + 1:P, :, P:D], x1[a:P - 1, :, P:D]).then_inc(h_in, 16)
                    sp.dma_start(hb[0:1, 1, P:D], x1[P - 1:P, 0, P:D]).then_inc(h_in, 16)

            run_steps(sp, step)
            sp.wait_ge(res_stored, 16 * STEPS)

        @block.tensor
        def _(pe):
            mm = nc.tensor.matmul

            def transpose_rows(src, b):
                for k in range(KC):
                    for t in range(T):
                        last = nc.tensor.transpose(bank(b)[:, k * S + t * P:k * S + t * P + P],
                                                   src[:, t, k * P:(k + 1) * P], ident[:])
                return last

            pe.wait_ge(cst_in, 16 * 10)
            pe.wait_ge(wx_in, 48)

            def project_T(w, src, b, done):
                for m in range(KC):
                    for k in range(KC):
                        last = mm(bank(b)[:, m * S:(m + 1) * S], w[:, k, m * P:(m + 1) * P],
                                  src[:, k, :], start=(k == 0), stop=(k == KC - 1))
                last.then_inc(done, 1)

            def turn(b, project, finish):
                if project:
                    pe.wait_ge(c_loaded, 16 * (b + 1))
                    wait(pe, cT_done, b)
                    transpose_rows(c_in, 0).then_inc(c_tr, 1)
                    pe.wait_ge(xn_done, T * (b + 1))
                    wait(pe, xnT_done, b)
                    transpose_rows(xn, 1).then_inc(xn_tr, 1)
                if finish:
                    pe.wait_ge(exp_x, T * b)
                    wait(pe, pT_x, b - 1)
                    for kt in range(T):
                        for qt in range(T):
                            last = nc.tensor.transpose(bank(6)[:, kt * S + qt * P:kt * S + qt * P + P],
                                                       xp[:, qt, kt * P:(kt + 1) * P], ident[:])
                    last.then_inc(p_tr, 1)
                if project:
                    pe.wait_ge(cT_done, b + 1)
                    wait(pe, kT_x, KC * b)
                    project_T(wk_sb, cT, 2, k_mm)
                if finish:
                    pe.wait_ge(pT_x, b)
                    pe.wait_ge(v_x, b)
                    wait(pe, xc_done, T * (b - 1))
                    for qt in range(T):
                        for kt in range(T):
                            last = mm(bank(7)[:, qt * D:(qt + 1) * D], xpT[:, kt, qt * P:(qt + 1) * P],
                                      xv[:, kt, :], start=(kt == 0), stop=(kt == T - 1))
                    last.then_inc(ctx_mm, 1)
                if project:
                    wait(pe, v_x, b)
                    for t in range(T):
                        for k in range(KC):
                            last = mm(bank(4)[:, t * D:(t + 1) * D], cT[:, k, t * P:(t + 1) * P],
                                      wv_sb[:, k, :], start=(k == 0), stop=(k == KC - 1))
                    last.then_inc(v_mm, 1)
                    pe.wait_ge(xnT_done, b + 1)
                    wait(pe, qT_x, KC * b)
                    project_T(wq_sb, xnT, 3, q_mm)
                    pe.wait_ge(kT_x, KC * (b + 1))
                    pe.wait_ge(qT_x, KC * (b + 1))
                    wait(pe, smax, T * b)
                    for qt in range(T):
                        for k in range(KC):
                            last = mm(bank(5)[:, qt * S:(qt + 1) * S], xqT[:, k, qt * P:(qt + 1) * P],
                                      xkT[:, k, :], start=(k == 0), stop=(k == KC - 1))
                    last.then_inc(s_mm, 1)

            run_x(pe, turn)

            pe.wait_ge(zeros_set, ZEROS)
            pe.wait_ge(ynext_in, 16)
            transpose_rows(y_next, 0).then_inc(y_tr, 1)

            def step(s, la, lf):
                f = s - 1

                def project(t):
                    i = 0 if t == 0 else 3
                    if t == 0:
                        pe.wait_ge(yT_done, s + 1)
                        if isinstance(s, int) and s in (0, NB):
                            pe.wait_ge(w0_in if la == 0 else w1_in, 16 * 5)
                    else:
                        wait(pe, pT_done, HEADS * s)
                    for j in range(3):
                        if j == 2:
                            if t == 0:
                                wait(pe, x1_done, s)
                            else:
                                pe.wait_ge(v_done, T * s + t)
                        o = bank(i + j) if j < 2 else bank(2)
                        for k in range(KC):
                            c0 = k * YTC - k + t * P
                            last = mm(o, yT[:, c0:c0 + P], wqkv_sb[la][:, k, j * INNER:(j + 1) * INNER],
                                      start=(k == 0), stop=(k == KC - 1))
                        if j:
                            last.then_inc((None, qk_mm, v_mm2)[j], 1)

                def up(c):
                    i, r = 5 + c % 2, hrows[c]
                    if c == 0:
                        pe.wait_ge(hT_done, KC * s)
                    if c < 2:
                        pe.wait_ge(o_done, PAIRS * s)
                    else:
                        pe.wait_ge(u_done, HC * f + c - 1)
                    for half in range(2):
                        o = half * HID + c * P
                        for k in range(KC):
                            last = mm(ps[0:r, i, half * S:(half + 1) * S], w1_sb[lf][:, k, o:o + r],
                                      hT[:, k, :], start=(k == 0), stop=(k == KC - 1))
                    last.then_inc(up_mm, 1)

                def tr_heads(t):
                    i = 0 if t == 0 else 3
                    pe.wait_ge(sq_done, T * s + t + 1)
                    for j in range(2):
                        pe.wait_ge((qs_done, ks_done)[j], T * s + t + 1)
                        for c in range(PAIRS):
                            last = nc.tensor.transpose(bank(i + j)[:, c * P:(c + 1) * P],
                                                       t1[:, t, j * INNER + c * P:j * INNER + (c + 1) * P],
                                                       ident[:])
                        last.then_inc(qk_tr, 1)

                def scores(h):
                    b = bank(h % NS)
                    if h >= NS:
                        pe.wait_ge(mx_done, T * (HEADS * s + h - NS + 1))
                    mm(b[:, 0:P], qz[:, h, 0:P], kT[:, h // 2, 0:P], start=True, stop=True)
                    mm(b[:, P:3 * P], qz[:, h, P:S], kT[:, h // 2, :], start=True, stop=True)\
                        .then_inc(s_mm2, 1)

                def tr_probs(h):
                    b, p = bank(3 + h % 2), pr[:, h % NS, :]
                    pe.wait_ge(pn_done, T * (HEADS * s + h + 1))
                    if h >= 2:
                        pe.wait_ge(pT_done, HEADS * s + h - 1)
                    nc.tensor.transpose(b[:, 0:P], p[:, 2 * P:3 * P], ident[:])
                    nc.tensor.transpose(b[:, P:2 * P], p[:, 0:P], ident[:])
                    nc.tensor.transpose(b[:, 2 * P:3 * P], p[:, P:2 * P], ident[:]).then_inc(pt_tr, 1)

                def weighted(h):
                    pair, j = h // 2, h % 2
                    b = bank(5 + pair % 2)
                    pe.wait_ge(pT_done, HEADS * s + h + 1)
                    if j == 0:
                        if pair < 2:
                            if lf is not None:
                                pe.wait_ge(u_done, HC * s)
                        else:
                            pe.wait_ge(o_done, PAIRS * s + pair - 1)
                    v = [vz[:, t, pair, j:j + 2, :].rearrange("p a d -> p (a d)") for t in range(T)]
                    mm(b[:, 0:S], v[0], pT[:, h % 2, P:3 * P], start=(j == 0), stop=False)
                    mm(b[:, P:S], v[1], pT[:, h % 2, 0:P], start=False, stop=(j == 1)).then_inc(pv_mm, 1)

                def down(n):
                    t, c = n // HC, n % HC
                    if n == 0:
                        pe.wait_ge(u_done, HC * s)
                    last = mm(bank(7)[:, t * D:(t + 1) * D], u[:, c, t * P:(t + 1) * P], w2_sb[lf][:, c, :],
                              start=(c == 0), stop=(c == HC - 1))
                    if n == T * HC - 1:
                        last.then_inc(dn_mm, 1)

                A, F = la is not None, lf is not None
                if A:
                    project(0)
                    project(1)
                if F:
                    pe.wait_ge(hn_done, s)
                    wait(pe, res_done, f)
                    transpose_rows(hn, 7).then_inc(h_tr, 1)
                    for c in range(4):
                        up(c)
                if A:
                    tr_heads(0)
                if F:
                    for c in range(4, HC):
                        up(c)
                if A:
                    tr_heads(1)
                    pe.wait_ge(q_done, 2 * T * (s + 1))
                    pe.wait_ge(k_done, T * (s + 1))
                    pe.wait_ge(v_done, T * (s + 1))
                    for h in range(NS):
                        scores(h)
                if A:
                    n = 0
                    for h in range(HEADS + 1):
                        if h < HEADS:
                            tr_probs(h)
                        if F:
                            while n * (HEADS + 1) < T * HC * (h + 1):
                                down(n)
                                n += 1
                        if h + NS < HEADS:
                            scores(h + NS)
                        if h:
                            weighted(h - 1)
                    pe.wait_ge(o_done, PAIRS * (s + 1))
                    for t in range(T):
                        for c in range(PAIRS):
                            last = mm(bank(2)[:, t * D:(t + 1) * D], oT[:, c, t * P:(t + 1) * P],
                                      wo_sb[la][:, c, :], start=(c == 0), stop=(c == PAIRS - 1))
                    last.then_inc(wo_mm, 1)
                    if not (isinstance(s, int) and s == STEPS - 1):
                        pe.wait_ge(ynext_in, 16 * (s + 2))
                        transpose_rows(y_next, 0).then_inc(y_tr, 1)
                elif F:
                    for n in range(T * HC):
                        down(n)

            run_steps(pe, step)

        @block.scalar
        def _(act):
            A = nc.scalar.activation
            act.wait_ge(cst_in, 16 * 10)
            A(tg[:], g_in[:], ACT.Tanh).then_inc(tanh_done, 1)

            def turn(b, project, finish):
                if project:
                    act.wait_ge(c_tr, b + 1)
                    wait(act, v_mm, b)
                    A(cT[:], halves(0), ACT.Copy).then_inc(cT_done, 1)
                    act.wait_ge(xn_tr, b + 1)
                    wait(act, q_mm, b)
                    A(xnT[:], halves(1), ACT.Copy).then_inc(xnT_done, 1)
                if finish:
                    act.wait_ge(p_tr, b)
                    wait(act, ctx_mm, b - 1)
                    A(xpT[:], halves(6), ACT.Copy).then_inc(pT_x, 1)
                if project:
                    for i, (mm_done, done, dst, j) in enumerate(((k_mm, kT_x, xkT, 1), (q_mm, qT_x, xqT, 0))):
                        act.wait_ge(mm_done, b + 1)
                        wait(act, s_mm, b)
                        for m in range(KC):
                            A(dst[:, m, :], halves(2 + i)[:, m, :], ACT.Identity,
                              bias=bqk[:, j, m:m + 1]).then_inc(done, 1)
                    act.wait_ge(nbx, b + 1)
                    wait(act, rlx, b)
                    for t in range(T):
                        A(xp[:, t, :], xs[:, t, :], ACT.Exp, bias=xnb[:, t:t + 1], scale=XSCALE,
                          accum_out=xl[:, t:t + 1]).then_inc(exp_x, 1)

            run_x(act, turn)

            def evac_yT(n):
                act.wait_ge(y_tr, n)
                dst = yT[:].rearrange("p (k c) -> p k c", c=YTC)[:, :, 0:S]
                A(dst, halves(0), ACT.Copy).then_inc(yT_done, 1)

            act.wait_ge(zeros_set, ZEROS)
            evac_yT(1)

            def step(s, la, lf):
                f = s - 1

                def squares(t):
                    act.wait_ge(qk_mm, T * s + t + 1)
                    wait(act, ss_done, T * s + t)
                    i = 0 if t == 0 else 3
                    A(sqb[:].rearrange("p (a n) -> p a n", a=2), ps[:, i:i + 2, :], ACT.Square)\
                        .then_inc(sq_done, 1)

                def values(t):
                    act.wait_ge(v_mm2, T * s + t + 1)
                    wait(act, pv_mm, HEADS * s)
                    A(vz[:, t, :, 0:3:2, :], bank(2).rearrange("p (a j d) -> p a j d", a=PAIRS, j=2),
                      ACT.Copy).then_inc(v_done, 1)

                def gelu(c):
                    act.wait_ge(up_mm, HC * f + c + 1)
                    wait(act, u_done, HC * f + max(0, c - 1))
                    r = hrows[c]
                    A(gl[0:r, c % 2, :], ps[0:r, 5 + c % 2, S:2 * S], ACT.Gelu,
                      bias=b1_sb[0:r, lf, 1, c:c + 1]).then_inc(gl_done, 1)

                def heads_T(t):
                    i = 0 if t == 0 else 3
                    act.wait_ge(qk_tr, 2 * (T * s + t) + 1)
                    wait(act, s_mm2, HEADS * s)
                    q = qz[:].rearrange("p (c j) n -> p c j n", j=2)
                    for j in range(2):
                        lo = j * DH
                        A(q[lo:lo + DH, :, j, t * P:(t + 1) * P],
                          ps[lo:lo + DH, i, :].rearrange("p (c n) -> p c n", c=PAIRS), ACT.Copy)\
                            .then_inc(q_done, 1)
                    act.wait_ge(qk_tr, 2 * (T * s + t) + 2)
                    A(kT[:, :, t * P:(t + 1) * P], bank(i + 1).rearrange("p (c n) -> p c n", c=PAIRS),
                      ACT.Copy).then_inc(k_done, 1)

                def exps(h):
                    act.wait_ge(nb_done, HEADS * s + h + 1)
                    if h >= NS:
                        act.wait_ge(pt_tr, HEADS * s + h - NS + 1)
                    wait(act, rl_done, HEADS * s)
                    for t, (a, b) in enumerate(((0, P), (P, 3 * P))):
                        A(pr[:, h % NS, a:b], sm[:, h % NS, a:b], ACT.Exp, bias=nb[:, h, t:t + 1],
                          scale=rn8[:, t, h:h + 1], accum_out=ls[:, h, t:t + 1]).then_inc(e_done, 1)

                def probs_T(h):
                    act.wait_ge(pt_tr, HEADS * s + h + 1)
                    wait(act, pv_mm, HEADS * s + h - 1)
                    A(pT[:, h % 2, :], bank(3 + h % 2)[:, 0:3 * P], ACT.Copy).then_inc(pT_done, 1)

                def heads_out(pair):
                    act.wait_ge(pv_mm, HEADS * s + 2 * pair + 2)
                    wait(act, wo_mm, s)
                    A(oT[:, pair, :], bank(5 + pair % 2)[:, 0:S], ACT.Copy).then_inc(o_done, 1)

                if la is not None:
                    for t in range(T):
                        squares(t)
                        values(t)
                if lf is not None:
                    act.wait_ge(h_tr, s)
                    wait(act, up_mm, HC * f)
                    for k in range(KC):
                        A(hT[:, k, :], halves(7)[:, k, :], ACT.Identity, scale=lgb[:, lf, 0, k:k + 1],
                          bias=lgb[:, lf, 1, k:k + 1]).then_inc(hT_done, 1)
                    for c in range(4):
                        gelu(c)
                if la is not None:
                    heads_T(0)
                if lf is not None:
                    for c in range(4, HC):
                        gelu(c)
                if la is not None:
                    heads_T(1)
                    exps(0)
                    for h in range(HEADS):
                        if h + 1 < HEADS:
                            exps(h + 1)
                        if h >= 2 and h % 2 == 0:
                            heads_out(h // 2 - 1)
                        probs_T(h)
                    heads_out(PAIRS - 1)
                    if not (isinstance(s, int) and s == STEPS - 1):
                        evac_yT(s + 2)

            run_steps(act, step)

        @block.vector
        def _(dve):
            V = nc.vector
            V.memset(yT[:], 0.0).then_inc(zeros_set, 1)
            V.memset(qz[:], 0.0).then_inc(zeros_set, 1)
            V.memset(vz[:], 0.0).then_inc(zeros_set, 1)
            V.memset(u[:], 0.0).then_inc(zeros_set, 1)
            V.memset(hb[:], 0.0).then_inc(zeros_set, 1)
            V.memset(nhalf[:], -0.5).then_inc(zeros_set, 1)
            for l in range(DEPTH):
                V.memset(w2_sb[l][:, HC - 1, :], 0.0).then_inc(zeros_set, 1)
            dve.wait_ge(cst_in, 16 * 10)
            dve.wait_ge(tanh_done, 1)
            V.tensor_scalar(gam_bc[:], gam_bc[:], tg[:, 0:1], None, ALU.mult).then_inc(prep_done, 1)
            V.tensor_scalar(bet_bc[:], bet_bc[:], tg[:, 0:1], None, ALU.mult).then_inc(prep_done, 1)

            def turn(b, project, finish):
                bn = xbn
                done_p = T * b + 2 * T * (b - 1) if finish else 0
                if project:
                    dve.wait_ge(x_loaded, 16 * (b + 1))
                    wait(dve, xvar, 0 if not finish else done_p)
                    for t in range(T):
                        V.bn_stats(xst[:, t, :], x_in[:, t, :]).then_inc(bn, 1)
                    for t in range(T):
                        wait_apart(dve, dve_passed, (bn, done_p + t + 1))
                        V.bn_aggr(xmv[:, 0, t, :], xst[:, t, :]).then_inc(xvar, 1)
                if project:
                    dve.wait_ge(xrstd, 3 * b - 1 if finish else 1)
                    wait(dve, xn_tr, b)
                    for t in range(T):
                        V.tensor_scalar(xn[:, t, :], x_in[:, t, :], xmv[:, 0, t, 0:1], xrs[:, 0, t:t + 1],
                                        ALU.subtract, ALU.mult).then_inc(xn_done, 1)
                if finish:
                    dve.wait_ge(ctx_mm, b)
                    dve.wait_ge(rlx, b)
                    wait(dve, tg_done, b - 1)
                    for t in range(T):
                        V.tensor_scalar(xc[:, t, :], halves(7)[:, t, :], xrl[:, t:t + 1], None,
                                        ALU.mult).then_inc(xc_done, 1)
                base = done_p + (T if project else 0)
                if finish:
                    dve.wait_ge(xc_done, T * b)
                    dve.wait_ge(xvar, base)
                    for t in range(T):
                        V.bn_stats(xst[:, t, :], xc[:, t, :]).then_inc(bn, 1)
                    for t in range(T):
                        wait_apart(dve, dve_passed, (bn, base + t + 1))
                        V.bn_aggr(xmv[:, 1, t, :], xst[:, t, :]).then_inc(xvar, 1)
                if project:
                    dve.wait_ge(m_loaded, 16 * (b + 1))
                    wait(dve, smax, T * b)
                    V.tensor_scalar(mbias[:], m_in[:], 0, NEG, ALU.is_equal, ALU.mult).then_inc(mb_done, 1)
                    dve.wait_ge(v_mm, b + 1)
                    V.tensor_tensor(xv[:], halves(4), bv_bc[:].unsqueeze(1).to_broadcast([P, T, D]),
                                    ALU.add).then_inc(v_x, 1)
                r0 = 3 * b - 2 if finish else 0
                if finish:
                    rs1 = r0 + (2 if project else 1)
                    dve.wait_ge(xrstd, rs1)
                    for t in range(T):
                        V.tensor_scalar(xc[:, t, :], xc[:, t, :], xmv[:, 1, t, 0:1], xrs[:, 1, t:t + 1],
                                        ALU.subtract, ALU.mult).then_inc(tn_done, 1)
                    dve.wait_ge(tn_done, T * b)
                    V.tensor_tensor(xc[:], xc[:], gam_bc[:].unsqueeze(1).to_broadcast([P, T, D]),
                                    ALU.mult).then_inc(tg_done, 1)
                    dve.wait_ge(tg_done, b)
                    dve.wait_ge(xrb_done, b)
                    wait(dve, xmid_stored, 16 * (b - 1))
                    V.tensor_tensor(x_mid[:], xc[:], x_res[:], ALU.add).then_inc(xmid_done, 1)
                    dve.wait_ge(xmid_done, b)
                    for t in range(T):
                        V.bn_stats(xst[:, t, :], x_mid[:, t, :]).then_inc(bn, 1)
                    for t in range(T):
                        wait_apart(dve, dve_passed, (bn, base + T + t + 1))
                        V.bn_aggr(xmv[:, 2, t, :], xst[:, t, :]).then_inc(xvar, 1)
                if project:
                    wait_apart(dve, dve_passed, (s_mm, b + 1),
                                               (mb_done, b + 1),
                                               (exp_x, T * b))
                    for t in range(T):
                        V.tensor_tensor_reduce(xs[:, t, :], halves(5)[:, t, :], mbias[:, t, :], 1.0, NEG,
                                               ALU.add, ALU.max, xmx[:, t:t + 1]).then_inc(smax, 1)
                    dve.wait_ge(smax, T * (b + 1))
                    V.tensor_scalar(xnb[:], xmx[:], -XSCALE, None, ALU.mult).then_inc(nbx, 1)
                if finish:
                    dve.wait_ge(xrstd, rs1 + 1)
                    wait(dve, y_stored, 16 * (b - 1))
                    for t in range(T):
                        V.tensor_scalar(y_new[:, t, :], x_mid[:, t, :], xmv[:, 2, t, 0:1], xrs[:, 2, t:t + 1],
                                        ALU.subtract, ALU.mult).then_inc(y_done_x, 1)
                if project:
                    dve.wait_ge(exp_x, T * (b + 1))
                    wait(dve, xc_done, T * b)
                    V.reciprocal(xrl[:], xl[:]).then_inc(rlx, 1)

            dve.wait_ge(prep_done, 2)
            run_x(dve, turn)

            dve.wait_ge(cst2_in, CONSTS)
            H = DH // 2
            for l in range(DEPTH):
                sc = qks[:, l, :].rearrange("p (a d) -> p a d", a=2).unsqueeze(1).to_broadcast([P, T, 2, DH])
                cos, sin = (rtab[:, :, i, :].rearrange("p t (a d) -> p t a d", a=2) for i in range(2))
                V.tensor_tensor(tc_sb[l][:], cos, sc, ALU.mult).then_inc(prep_done, 1)
                V.tensor_tensor(ts_sb[l][:, :, :, 0:H], sin[:, :, :, 0:H], sc[:, :, :, H:DH],
                                ALU.mult).then_inc(prep_done, 1)
                V.tensor_tensor(ts_sb[l][:, :, :, H:DH], sin[:, :, :, H:DH], sc[:, :, :, 0:H],
                                ALU.mult).then_inc(prep_done, 1)
            dve.wait_ge(prep_done, 2 + 3 * DEPTH)
            dve.wait_ge(zeros_set, ZEROS)

            def step(s, la, lf):
                f = s - 1

                def rotate(t):
                    i = 0 if t == 0 else 3
                    dve.wait_ge(sq_done, T * s + t + 1)
                    wait(dve, qk_tr, 2 * (T * (s - 1) + t + 1) if not isinstance(s, int) or s else 0)
                    wait(dve, ka_done, T * (s - 1) + t + 1 if not isinstance(s, int) or s else 0)
                    qk = ps[:, i:i + 2, :].rearrange("p a (h d) -> p a h d", d=DH)
                    a1, a2 = (b[:, t, :].rearrange("p (a h d) -> p a h d", a=2, d=DH) for b in (t1, t2))
                    tc = tc_sb[la][:, t].unsqueeze(2).to_broadcast([P, 2, HEADS, DH])
                    ts = ts_sb[la][:, t].unsqueeze(2).to_broadcast([P, 2, HEADS, DH])
                    V.tensor_tensor(a1, qk, tc, ALU.mult)
                    V.tensor_tensor(a2[:, :, :, 0:H], qk[:, :, :, H:DH], ts[:, :, :, 0:H], ALU.mult)
                    V.tensor_tensor(a2[:, :, :, H:DH], qk[:, :, :, 0:H], ts[:, :, :, H:DH], ALU.mult)\
                        .then_inc(rot_done, 1)

                def norms(t):
                    wait(dve, rn_done, T * (s - 1) + t + 1 if not isinstance(s, int) or s else 0)
                    V.tensor_reduce(ss[:, t, :], sqb[:].rearrange("p (h d) -> p h d", d=DH), AX.X,
                                    ALU.add).then_inc(ss_done, 1)

                def gated(c):
                    dve.wait_ge(gl_done, HC * f + c + 1)
                    wait(dve, dn_mm, f)
                    r = hrows[c]
                    V.scalar_tensor_tensor(u[0:r, c, :], ps[0:r, 5 + c % 2, 0:S], b1_sb[0:r, lf, 0, c:c + 1],
                                           gl[0:r, c % 2, :], ALU.add, ALU.mult).then_inc(u_done, 1)

                def row_max(h):
                    wait_apart(dve, dve_passed, (s_mm2, HEADS * s + h + 1),
                               (e_done, T * (HEADS * s + max(0, h - NS + 1))),
                               (nb_done, HEADS * s))
                    for t, (a, b) in enumerate(((0, P), (P, 3 * P))):
                        V.tensor_tensor_reduce(sm[:, h % NS, a:b], bank(h % NS)[:, a:b], wmask[:, a:b], 1.0,
                                               NEG, ALU.add, ALU.max, mx[:, h, t:t + 1]).then_inc(mx_done, 1)
                    dve.wait_ge(mx_done, T * (HEADS * s + h + 1))
                    dve.wait_ge(rn8_done, 2 * T * (s + 1))
                    V.tensor_tensor(nb[:, h, :], mx[:, h, :], nrn8[:, :, h], ALU.mult).then_inc(nb_done, 1)

                def row_sum(h):
                    dve.wait_ge(e_done, T * (HEADS * s + h + 1))
                    wait(dve, pn_done, T * HEADS * s)
                    V.reciprocal(rl[:, h, :], ls[:, h, :]).then_inc(rl_done, 1)

                A, F = la is not None, lf is not None
                if F:
                    dve.wait_ge(h_in, 64 * s)
                    for t in range(T):
                        V.bn_stats(hst[:, t, :], hb[:, t, :]).then_inc(hbn_a, 1)
                    wait(dve, heps, f)
                    for t in range(T):
                        wait_apart(dve, dve_passed, (hbn_a, T * f + t + 1))
                        V.bn_aggr(hmv[:, t, :], hst[:, t, :]).then_inc(hbn, 1)
                if A:
                    rotate(0)
                    norms(0)
                if F:
                    dve.wait_ge(hrstd, s)
                    wait(dve, h_tr, f)
                    for t in range(T):
                        last = V.tensor_scalar(hn[:, t, :], hb[:, t, :], hmv[:, t, 0:1], hrs[:, t:t + 1],
                                               ALU.subtract, ALU.mult)
                    last.then_inc(hn_done, 1)
                if A:
                    rotate(1)
                    norms(1)
                if F:
                    for c in range(HC):
                        gated(c)
                if A:
                    row_max(0)
                    row_max(1)
                    for h in range(HEADS):
                        row_sum(h)
                        if h + 2 < HEADS:
                            row_max(h + 2)
                if F:
                    dve.wait_ge(dn_mm, s)
                    dve.wait_ge(xb_done, s)
                    wait(dve, res_stored, 16 * f)
                    V.tensor_tensor(yo[:], halves(7), x1b[:], ALU.add).then_inc(yo_done if lf else res_done, 1)
                    if lf == 1:
                        dve.wait_ge(yo_done, s - NB)
                        dve.wait_ge(xm_in, 16 * (s - NB))
                        V.scalar_tensor_tensor(flat(yo), flat(yo), tg[:, 1:2], flat(xm_res),
                                               ALU.mult, ALU.add).then_inc(res_done, 1)
                if A:
                    dve.wait_ge(wo_mm, s + 1)
                    dve.wait_ge(yres_in, 16 * (s + 1))
                    wait(dve, h_in, 64 * s)
                    wait(dve, xb_done, s)
                    V.tensor_tensor(x1[:], halves(2), y_res[:], ALU.add).then_inc(x1_done, 1)

            run_steps(dve, step)

        @block.gpsimd
        def _(pool):
            G = nc.gpsimd
            pool.wait_ge(zeros_set, ZEROS)
            pool.wait_ge(prep_done, 2)
            def rstd(var, dst, a, b, after_a):
                G.tensor_scalar(dst, var, LN_EPS, 1.0, ALU.add, ALU.mult).then_inc(a, 1)
                pool.wait_ge(a, after_a)
                G.tensor_tensor(dst, dst, nhalf[:, 0:T], ALU.pow).then_inc(b, 1)

            def turn(b, project, finish):
                v0 = T * b + 2 * T * (b - 1) if finish else 0
                r0 = 3 * b - 2 if finish else 0
                if project:
                    wait_apart(pool, pool_passed, (xvar, v0 + T),
                                                (xn_done, T * b))
                    rstd(xmv[:, 0, :, 1], xrs[:, 0, :], xrstd_a, xrstd, r0 + 1)
                    v0, r0 = v0 + T, r0 + 1
                if finish:
                    wait_apart(pool, pool_passed, (xvar, v0 + T))
                    rstd(xmv[:, 1, :, 1], xrs[:, 1, :], xrstd_a, xrstd, r0 + 1)
                    pool.wait_ge(xres_loaded, 16 * b)
                    G.tensor_tensor(x_res[:], x_res[:], bet_bc[:].unsqueeze(1).to_broadcast([P, T, D]),
                                    ALU.add).then_inc(xrb_done, 1)
                    wait_apart(pool, pool_passed, (xvar, v0 + 2 * T),
                                                (y_done_x, T * (b - 1)))
                    rstd(xmv[:, 2, :, 1], xrs[:, 2, :], xrstd_a, xrstd, r0 + 2)

            run_x(pool, turn)
            pool.wait_ge(cst2_in, CONSTS)

            def step(s, la, lf):
                f = s - 1

                def inverse_norms(t):
                    wait_apart(pool, pool_passed, (ss_done, T * s + t + 1))
                    G.tensor_scalar(ss[:, t, :], ss[:, t, :], L2_EPS2, 1.0, ALU.max, ALU.mult)\
                        .then_inc(ssc_done, 1)
                    pool.wait_ge(ssc_done, T * s + t + 1)
                    wait(pool, e_done, T * HEADS * s)
                    G.tensor_tensor(rn[:, t, :], ss[:, t, :], nhalf[:], ALU.pow).then_inc(rn_done, 1)
                    wait_apart(pool, pool_passed, (rn_done, T * s + t + 1))
                    G.tensor_scalar(rn8[:, t, :], rn[:, t, 0:HEADS], QK_SCALE, 1.0, ALU.mult, ALU.mult)\
                        .then_inc(rn8_done, 1)
                    G.tensor_scalar(nrn8[:, t, :], rn[:, t, 0:HEADS], -QK_SCALE, 1.0, ALU.mult, ALU.mult)\
                        .then_inc(rn8_done, 1)

                def rotary_sum(t):
                    pool.wait_ge(rot_done, T * s + t + 1)
                    q, k = (slice(j * INNER, (j + 1) * INNER) for j in range(2))
                    G.tensor_tensor(t1[:, t, q], t1[:, t, q], t2[:, t, q], ALU.add).then_inc(qs_done, 1)
                    G.tensor_tensor(t1[:, t, k], t1[:, t, k], t2[:, t, k], ALU.add).then_inc(ka_done, 1)
                    pool.wait_ge(ka_done, T * s + t + 1)
                    kh = t1[:, t, k].rearrange("p (h d) -> p h d", d=DH)
                    rk = rn[:, t, HEADS:2 * HEADS].unsqueeze(2).to_broadcast([P, HEADS, DH])
                    G.tensor_tensor(kh, kh, rk, ALU.mult).then_inc(ks_done, 1)

                def normalise(h):
                    wait_apart(pool, pool_passed, (rl_done, HEADS * s + h + 1))
                    for t, (a, b) in enumerate(((0, P), (P, 3 * P))):
                        G.tensor_scalar(pr[:, h % NS, a:b], pr[:, h % NS, a:b], rl[:, h, t:t + 1], 1.0,
                                        ALU.mult, ALU.mult).then_inc(pn_done, 1)

                if lf is not None:
                    wait_apart(pool, pool_passed, (hbn, T * s),
                                                (hn_done, f))
                    rstd(hmv[:, :, 1], hrs[:], heps, hrstd, s)
                if la is not None:
                    inverse_norms(0)
                    rotary_sum(0)
                    inverse_norms(1)
                    rotary_sum(1)
                if lf is not None:
                    pool.wait_ge(x1_done, s)
                    wait(pool, res_done, f)
                    G.tensor_tensor(x1b[:], x1[:], b2_bc[lf][:].unsqueeze(1).to_broadcast([P, T, D]),
                                    ALU.add).then_inc(xb_done, 1)
                if la is not None:
                    for h in range(HEADS):
                        normalise(h)

            run_steps(pool, step)


CONSTS = 16 * 18
ZEROS = 6 + 2


def host_tables(S):
    import numpy as np
    half = np.arange(0, DH, 2, dtype=np.float32)
    inv = (np.float32(1.0) / np.float32(10000.0) ** (half / np.float32(DH))).astype(np.float32)
    t = np.arange(S, dtype=np.float32)
    fr = t[:, None] * inv[None, :]
    base = (half + np.float32(0.4 * DH)) / np.float32(1.4 * DH)
    power = (t - S // 2) / np.float32(64)
    sc = base[None, :].astype(np.float64) ** power[:, None].astype(np.float64)
    cos, sin = np.cos(fr.astype(np.float64)), np.sin(fr.astype(np.float64))

    def both(a, b):
        return np.concatenate([a, b], axis=1)
    tab = np.stack([both(both(cos * sc, cos * sc), both(cos / sc, cos / sc)),
                    both(both(-sin * sc, sin * sc), both(-sin / sc, sin / sc))], axis=1)
    tab = tab.reshape(S // P, P, 2, 2 * DH).transpose(1, 0, 2, 3)
    i, j = np.arange(P)[:, None], np.arange(P)[None, :]
    own, prev = np.where(j <= i, 0.0, NEG), np.where(j >= i, 0.0, NEG)
    return (np.ascontiguousarray(tab, np.float32),
            np.concatenate([own, prev, own], axis=1).astype(np.float32), np.eye(P, dtype=np.float32))


_INS = ['x', 'ctx_1024', 'mask_BxSxS2_ik1', 'g_xattn', 'g_ffn', 'L0_xattn_Wq', 'L0_xattn_bq', 'L0_xattn_Wk',
        'L0_xattn_bk', 'L0_xattn_Wv', 'L0_xattn_bv', 'L0_xattn_ln_gamma', 'L0_xattn_ln_beta', 'L0_ffn_wqkv',
        'L0_ffn_q_scale', 'L0_ffn_k_scale', 'L0_ffn_wo', 'L0_ffn_ln_g', 'L0_ffn_ln_b', 'L0_ffn_w1',
        'L0_ffn_b1', 'L0_ffn_w2', 'L0_ffn_b2']


def kernel(**inputs):
    import numpy as np
    import concourse.bacc as bacc
    from concourse.bass_utils import run_bass_kernel_spmd

    arrays = {n: np.ascontiguousarray(inputs[n]) for n in _INS}
    tab, win, eye = host_tables(arrays['x'].shape[1])
    arrays.update(rot_tab=tab, win_mask=win, identity=eye)
    nc = bacc.Bacc("TRN2", target_bir_lowering=False, num_devices=1)
    args = [nc.dram_tensor(n, a.shape, mybir.dt.from_np(a.dtype), kind="ExternalInput").ap()
            for n, a in arrays.items()]
    out = nc.dram_tensor("out", arrays['x'].shape, F32, kind="ExternalOutput").ap()
    build(nc, *args, out)
    r = run_bass_kernel_spmd(nc, [arrays], core_ids=[0])
    return r.results[0]["out"]
```

```python
from contextlib import ExitStack

import concourse.bass as bass
from concourse import mybir

P = 128
F32 = mybir.dt.float32
F32R = mybir.dt.float32r
I32 = mybir.dt.int32
ALU = mybir.AluOpType
ACT = mybir.ActivationFunctionType
AX = mybir.AxisListType

NEG = -1.0e30
LN_EPS = 1e-5
L2_EPS2 = 1e-24
HEADS, DH = 8, 64
QK_SCALE = 8.0
FMAX_DMA = 16


def wait(eng, semaphore, value):
    if isinstance(value, int) and value <= 0:
        return
    eng.wait_ge(semaphore, value)


def wait_apart(eng, passed, *waits):
    for semaphore, value in waits:
        wait(eng, semaphore, value)
    eng.sem_inc(passed, 1)


def build(nc, x, ctx_in, mask, g_xattn, g_ffn, Wq, bq, Wk, bk, Wv, bv, ln_gamma, ln_beta,
          wqkv, q_scale, k_scale, wo, ln_g, ln_b, w1, b1, w2, b2, rot_tab, win_mask, ident_in, shift_in, out):
    NB, S, D = x.shape
    T = S // P
    KC = D // P
    DEPTH = wqkv.shape[0]
    INNER = HEADS * DH
    PAIRS = HEADS // 2
    HID = w2.shape[1]
    HC = (HID + P - 1) // P
    HT = HID - (HC - 1) * P
    hrows = [P] * (HC - 1) + [HT]
    STEPS = DEPTH * NB
    XSCALE = float(D) ** -0.5
    YTC = S + 3
    NS = 3
    assert S == 2 * P and D == 2 * P and DEPTH == 2

    xmid = nc.dram_tensor("xmid", [NB, P, T * D], F32, kind="Internal").ap()
    ystream = nc.dram_tensor("ystream", [STEPS, P, T * D], F32, kind="Internal").ap()

    st = ExitStack()
    with st:
        def sb(name, shape, dt=F32):
            return st.enter_context(nc.sbuf_tensor(name, shape, dt))

        def sem(name):
            return st.enter_context(nc.semaphore(name))

        wqkv_hl = [sb(f"wqkv_{n}", [P, KC, 3 * INNER], F32R) for n in ("hi", "lo")]
        wo_hl = [sb(f"wo_{n}", [P, PAIRS, D], F32R) for n in ("hi", "lo")]
        w1_hl = [sb(f"w1_{n}", [P, KC, 2 * HID], F32R) for n in ("hi", "lo")]
        w2_hl = [sb(f"w2_{n}", [P, HC, D], F32R) for n in ("hi", "lo")]
        ident = sb("ident", [P, P])
        shift = sb("shift", [P, 2 * P])
        wmask = sb("wmask", [P, 3 * P])
        rtab = sb("rtab", [P, T, 2, 2 * DH])
        qks = sb("qks", [P, DEPTH, 2 * DH])
        tc_sb = [sb(f"tc_sb{l}", [P, T, 2, DH]) for l in range(DEPTH)]
        ts_sb = [sb(f"ts_sb{l}", [P, T, 2, DH]) for l in range(DEPTH)]
        bqk = sb("bqk", [P, 2, KC])
        bv_bc = sb("bv_bc", [P, D])
        gam_bc = sb("gam_bc", [P, D])
        bet_bc = sb("bet_bc", [P, D])
        b2_bc = [sb(f"b2_bc{l}", [P, D]) for l in range(DEPTH)]
        lgb = sb("lgb", [P, DEPTH, 2, KC])
        b1_sb = sb("b1_sb", [P, DEPTH, 2, HC])
        g_in = sb("g_in", [P, 2])
        tg = sb("tg", [P, 2])
        nhalf = sb("nhalf", [P, 2 * HEADS])

        XTILES = 17
        arena = sb("arena", [P, XTILES + 3, T * D])
        x_in, c_in, m_raw, x_res, xn, xnT, cT, xqT, xkT, xv, mbias, xs, xp, xpT, xc, x_mid, y_new = (
            arena[:, i, :].rearrange("p (t d) -> p t d", t=T) for i in range(XTILES))
        m_in = m_raw.bitcast(I32)
        wq_sb, wk_sb, wv_sb = (arena[:, XTILES + i, :].rearrange("p (k d) -> p k d", k=KC) for i in range(3))
        x1b, yo, xm_res = (arena[:, XTILES + i, :].rearrange("p (t d) -> p t d", t=T) for i in range(3))
        raw = arena[:, 0:XTILES, :].rearrange("p i n -> p (i n)")
        cols = [0]
        for c in (KC * 3 * INNER, PAIRS * D, KC * 2 * HID, HC * D):
            cols.append(cols[-1] + c)
        assert cols[-1] <= XTILES * T * D
        wqkv_raw, wo_raw, w1_raw, w2_raw = (
            raw[:, cols[i]:cols[i + 1]].rearrange("p (k n) -> p k n", k=k)
            for i, k in enumerate((KC, PAIRS, KC, HC)))
        xst = sb("xst", [P, 3, T, 6])
        xmv = sb("xmv", [P, 3, T, 2])
        xrs = sb("xrs", [P, 3, T])
        xmx, xnb, xl, xrl = (sb(n, [P, T]) for n in ("xmx", "xnb", "xl", "xrl"))

        y_next = sb("y_next", [P, T, D])
        y_res = sb("y_res", [P, T, D])
        yT = [sb(f"yT_{n}", [P, KC * YTC], F32R) for n in ("hi", "lo")]
        turned = sb("turned", [P, 3 * 2 * INNER])
        t1 = turned[:, 0:T * 2 * INNER].rearrange("p (t n) -> p t n", t=T)
        t2 = turned[:, T * 2 * INNER:3 * 2 * INNER]
        sqb = sb("sqb", [P, 2 * INNER])
        ss = sb("ss", [P, T, 2 * HEADS])
        rn = sb("rn", [P, T, 2 * HEADS])
        rn8 = sb("rn8", [P, T, HEADS])
        nrn8 = sb("nrn8", [P, T, HEADS])
        qz = sb("qz", [P, HEADS, S])
        kT = sb("kT", [P, PAIRS, S])
        vz = sb("vz", [P, T, PAIRS, 3, DH])
        sm = sb("sm", [P, NS, 3 * P])
        pr = sb("pr", [P, NS, 3 * P])
        pT = sb("pT", [P, 2, 3 * P])
        mx, nb, ls, rl = (sb(n, [P, HEADS, T]) for n in ("mx", "nb", "ls", "rl"))
        oT = [sb(f"oT_{n}", [P, PAIRS, S], F32R) for n in ("hi", "lo")]
        x1 = sb("x1", [P, T, D])
        hst = sb("hst", [P, T, 2, 6])
        hmv = sb("hmv", [P, T, 2])
        hrs = sb("hrs", [P, T])
        hn = sb("hn", [P, T, D])
        hT = [sb(f"hT_{n}", [P, KC, S], F32R) for n in ("hi", "lo")]
        gl = sb("gl", [P, 2, S])
        u_full = sb("u_full", [P, 2, S])
        u = [sb(f"u_{n}", [P, HC, S], F32R) for n in ("hi", "lo")]

        ps = st.enter_context(nc.psum_tensor("ps", [P, 8, 512], F32))

        def bank(i):
            return ps[:, i, :]

        def halves(i):
            return ps[:, i, :].rearrange("p (t n) -> p t n", t=2)

        ident_loaded, wx_in, cst_in, cst2_in, wa_in, wb_in = (
            sem(n) for n in ("ident_loaded", "wx_in", "cst_in", "cst2_in", "wa_in", "wb_in"))
        w_high, w_ready = sem("w_high"), sem("w_ready")
        b1_mm, b1_done, w1_scaled = sem("b1_mm"), sem("b1_done"), sem("w1_scaled")
        zeros_set, tanh_done, prep_done = sem("zeros_set"), sem("tanh_done"), sem("prep_done")
        dve_passed, pool_passed = sem("dve_passed"), sem("pool_passed")
        x_loaded, c_loaded, m_loaded, xres_loaded = (
            sem(n) for n in ("x_loaded", "c_loaded", "m_loaded", "xres_loaded"))
        xmid_stored, y_stored = sem("xmid_stored"), sem("y_stored")
        stats, var, eps_add, rstd_done = (
            [sem(f"{n}_{k}") for k in ("x", "ctx", "mid")] for n in ("stats", "var", "eps", "rstd"))
        (xn_done, c_tr, xn_tr, cT_done, xnT_done, k_mm, q_mm, v_mm, kT_x, qT_x,
         v_x, s_mm, mb_done, smax, nbx, exp_x, rlx, p_tr, pT_x, ctx_mm, xc_done, tn_done, tg_done,
         xmid_done, xrb_done, y_done_x) = (sem(n) for n in (
             "xn_done", "c_tr", "xn_tr", "cT_done", "xnT_done", "k_mm", "q_mm",
             "v_mm", "kT_x", "qT_x", "v_x", "s_mm", "mb_done", "smax", "nbx", "exp_x", "rlx", "p_tr",
             "pT_x", "ctx_mm", "xc_done", "tn_done", "tg_done", "xmid_done", "xrb_done", "y_done_x"))
        ynext_in, yres_in, xm_in, res_stored = (
            sem(n) for n in ("ynext_in", "yres_in", "xm_in", "res_stored"))
        (y_tr, sh_mm, yT_high, yT_done, qk_mm, v_mm2, sq_done, ss_done, ssc_done, rn_done, rn8_done, rot_done, sum_done,
         ks_done, v_done, o_high, hT_high, u_raw, u_high, qk_tr, q_done, k_done, s_mm2, mx_done, nb_done, e_done, rl_done,
         pn_done, pt_tr, pT_done, pv_mm, o_done, wo_mm, x1_done, hbn_a, hbn, heps, hrstd, hn_done, h_tr,
         hT_done, up_mm, gl_done, u_done, xb_done, dn_mm, yo_done, res_done) = (sem(n) for n in (
             "y_tr", "sh_mm", "yT_high", "yT_done", "qk_mm", "v_mm2", "sq_done", "ss_done", "ssc_done", "rn_done",
             "rn8_done", "rot_done", "sum_done", "ks_done", "v_done", "o_high", "hT_high", "u_raw",
             "u_high", "qk_tr", "q_done", "k_done", "s_mm2",
             "mx_done", "nb_done", "e_done", "rl_done", "pn_done", "pt_tr", "pT_done", "pv_mm", "o_done",
             "wo_mm", "x1_done", "hbn_a", "hbn", "heps", "hrstd", "hn_done", "h_tr", "hT_done", "up_mm",
             "gl_done", "u_done", "xb_done", "dn_mm", "yo_done", "res_done"))

        block = st.enter_context(nc.Block())

        def rows(ap):
            return ap.rearrange("(t p) d -> p t d", p=P)

        def flat(t):
            return t[:].rearrange("p t d -> p (t d)")

        def run_x(eng, turn, before_last=None):
            turn(0, True, False, True)
            turn(1, True, True, True)
            with eng.Fori(2, NB - 1) as b:
                turn(b, True, True, True)
            turn(NB - 1, True, True, False)
            if before_last:
                before_last()
            turn(NB, False, True, False)

        FIRST, PIECES = 4, 8

        def raws(l):
            if l == 0:
                return [turned[:].rearrange("p (k n) -> p k n", k=KC), kT[:], w1_raw, w2_raw]
            return [wqkv_raw, wo_raw, w1_raw, w2_raw]

        def pieces(l, first):
            full = raws(l)
            found = []
            if first:
                for j in range(3):
                    c = slice(j * INNER, (j + 1) * INNER)
                    found.append((full[0][:, :, c], wqkv_hl[0][:, :, c], wqkv_hl[1][:, :, c]))
                found.append((full[1], wo_hl[0][:], wo_hl[1][:]))
            else:
                for k in range(KC):
                    found.append((full[2][:, k, :], w1_hl[0][:, k, :], w1_hl[1][:, k, :]))
                for c, r in ((slice(0, HC - 1), P), (slice(HC - 1, HC), HT)):
                    found.append((full[3][0:r, c, :], w2_hl[0][0:r, c, :], w2_hl[1][0:r, c, :]))
            return found

        def run_steps(eng, step):
            step(0, 0, None)
            step(1, 0, 0)
            with eng.Fori(2, NB) as s:
                step(s, 0, 0)
            step(NB, 1, 0)
            with eng.Fori(NB + 1, STEPS - 1) as s:
                step(s, 1, 1)
            step(STEPS - 1, 1, 1)
            step(STEPS, None, 1)

        @block.sync
        def _(sp):
            def load_x(b):
                sp.dma_start(x_in, rows(x[b])).then_inc(x_loaded, 16)

            def load_c(b):
                sp.dma_start(c_in, rows(ctx_in[b])).then_inc(c_loaded, 16)

            def load_m(b):
                sp.dma_start(m_in, rows(mask[b])).then_inc(m_loaded, 16)

            sp.dma_start(ident[:], ident_in).then_inc(ident_loaded, 16)
            load_c(0)
            load_x(0)
            for w, dst in ((Wk, wk_sb), (Wv, wv_sb), (Wq, wq_sb)):
                sp.dma_start(dst, w.rearrange("(k p) n -> p k n", p=P)).then_inc(wx_in, 16)
            load_m(0)
            small = [(bqk[:, 0, :], bq.rearrange("(m p) -> p m", p=P)),
                     (bqk[:, 1, :], bk.rearrange("(m p) -> p m", p=P)),
                     (bv_bc[:], bv.partition_broadcast(P)),
                     (gam_bc[:], ln_gamma.partition_broadcast(P)),
                     (bet_bc[:], ln_beta.partition_broadcast(P)),
                     (g_in[:, 0:1], g_xattn.partition_broadcast(P)),
                     (g_in[:, 1:2], g_ffn.partition_broadcast(P)),
                     (shift[:], shift_in), (wmask[:], win_mask), (rtab[:], rot_tab)]
            for l in range(DEPTH):
                small += [(b2_bc[l][:], b2[l, :].partition_broadcast(P)),
                          (qks[:, l, 0:DH], q_scale[l, :].partition_broadcast(P)),
                          (qks[:, l, DH:2 * DH], k_scale[l, :].partition_broadcast(P)),
                          (lgb[:, l, 0, :], ln_g[l, :].rearrange("(k p) -> p k", p=P)),
                          (lgb[:, l, 1, :], ln_b[l, :].rearrange("(k p) -> p k", p=P))]
                for half in range(2):
                    o = half * HID
                    small += [(b1_sb[:, l, half, 0:HC - 1],
                               b1[l, o:o + HID - HT].rearrange("(c p) -> p c", p=P)),
                              (b1_sb[0:HT, l, half, HC - 1:HC],
                               b1[l, o + HID - HT:o + HID].unsqueeze(1))]
            assert 16 * len(small[7:]) == CONSTS
            for dst, src in small[:7]:
                sp.dma_start(dst, src, allow_slow_non_contiguous=True).then_inc(cst_in, 16)

            def load_layer(l, first):
                wqkv_to, wo_to, w1_to, w2_to = raws(l)
                if first:
                    sp.dma_start(wqkv_to, wqkv[l].rearrange("(k p) n -> p k n", p=P)).then_inc(wa_in, 16)
                    sp.dma_start(wo_to, wo[l].rearrange("(k p) n -> p k n", p=P)).then_inc(wa_in, 16)
                else:
                    sp.dma_start(w1_to, w1[l].rearrange("(k p) n -> p k n", p=P)).then_inc(wb_in, 16)
                    sp.dma_start(w2_to[:, 0:HC - 1, :],
                                 w2[l, 0:HID - HT, :].rearrange("(c p) n -> p c n", p=P)).then_inc(wb_in, 16)
                    sp.dma_start(w2_to[0:HT, HC - 1, :], w2[l, HID - HT:HID, :]).then_inc(wb_in, 16)

            def turn(b, project, finish, ahead):
                if ahead:
                    sp.wait_ge(xn_done, T * (b + 1))
                    load_x(b + 1)
                if finish:
                    wait(sp, xmid_done, b - 1)
                    sp.dma_start(x_res, rows(x[b - 1])).then_inc(xres_loaded, 16)
                if ahead:
                    sp.wait_ge(c_tr, b + 1)
                    load_c(b + 1)
                    sp.wait_ge(mb_done, b + 1)
                    load_m(b + 1)
                if finish:
                    sp.wait_ge(xmid_done, b)
                    sp.dma_start(xmid[b - 1], arena[:, 15, :]).then_inc(xmid_stored, 16)
                    sp.wait_ge(y_done_x, T * b)
                    sp.dma_start(ystream[b - 1], arena[:, 16, :]).then_inc(y_stored, 16)
                if isinstance(b, int) and b == 1:
                    for dst, src in small[7:]:
                        sp.dma_start(dst, src, allow_slow_non_contiguous=True).then_inc(cst2_in, 16)
                    load_layer(0, True)

            run_x(sp, turn)

            sp.wait_ge(y_stored, 16)
            sp.dma_start(flat(y_next), ystream[0]).then_inc(ynext_in, 16)
            sp.wait_ge(y_stored, 16 * NB)
            sp.wait_ge(xmid_stored, 16 * NB)

            def step(s, la, lf):
                f = s - 1
                if isinstance(s, int) and s == 0:
                    load_layer(0, False)
                if isinstance(s, int) and s == 1:
                    sp.wait_ge(w_ready, PIECES)
                    load_layer(1, True)
                    load_layer(1, False)
                if la is not None:
                    wait(sp, x1_done, s)
                    sp.dma_start(flat(y_res), ystream[s]).then_inc(yres_in, 16)
                    if not (isinstance(s, int) and s == STEPS - 1):
                        wait(sp, y_tr, s + 1)
                        if la == 0:
                            wait(sp, res_stored, 16 * f)
                        else:
                            sp.wait_ge(res_stored, 16 * (s + 2 - NB))
                        sp.dma_start(flat(y_next), ystream[s + 1]).then_inc(ynext_in, 16)
                if lf == 1:
                    sp.wait_ge(res_done, f)
                    sp.dma_start(arena[:, XTILES + 2, :], xmid[f - NB]).then_inc(xm_in, 16)
                if lf is not None:
                    sp.wait_ge(res_done, s)
                    sp.dma_start(rows(out[f - NB]) if lf else ystream[f + NB].rearrange("p (t d) -> p t d", t=T),
                                 yo).then_inc(res_stored, 16)

            run_steps(sp, step)
            sp.wait_ge(res_stored, 16 * STEPS)

        @block.tensor
        def _(pe):
            mm = nc.tensor.matmul

            def transpose_rows(src, b):
                for k in range(KC):
                    for t in range(T):
                        last = nc.tensor.transpose(bank(b)[:, k * S + t * P:k * S + t * P + P],
                                                   src[:, t, k * P:(k + 1) * P], ident[:])
                return last

            def split_product(out, lhsT, rhs, start, stop):
                for i, (a, b) in enumerate(((0, 0), (0, 1), (1, 0))):
                    last = mm(out, lhsT(a), rhs(b), start=(start and i == 0), stop=(stop and i == 2))
                return last

            pe.wait_ge(ident_loaded, 16)

            def project_T(w, src, b, done):
                for m in range(KC):
                    for k in range(KC):
                        last = mm(bank(b)[:, m * S:(m + 1) * S], w[:, k, m * P:(m + 1) * P],
                                  src[:, k, :], start=(k == 0), stop=(k == KC - 1))
                last.then_inc(done, 1)

            def turn(b, project, finish, ahead):
                if project:
                    pe.wait_ge(c_loaded, 16 * (b + 1))
                    wait(pe, cT_done, b)
                    transpose_rows(c_in, 0).then_inc(c_tr, 1)
                    pe.wait_ge(xn_done, T * (b + 1))
                    wait(pe, xnT_done, b)
                    transpose_rows(xn, 1).then_inc(xn_tr, 1)
                    if isinstance(b, int) and b == 0:
                        pe.wait_ge(wx_in, 48)
                    pe.wait_ge(cT_done, b + 1)
                    wait(pe, kT_x, KC * b)
                    project_T(wk_sb, cT, 2, k_mm)
                    wait(pe, v_x, b)
                    for t in range(T):
                        for k in range(KC):
                            last = mm(bank(4)[:, t * D:(t + 1) * D], cT[:, k, t * P:(t + 1) * P],
                                      wv_sb[:, k, :], start=(k == 0), stop=(k == KC - 1))
                    last.then_inc(v_mm, 1)
                if finish:
                    pe.wait_ge(exp_x, T * b)
                    wait(pe, pT_x, b - 1)
                    for kt in range(T):
                        for qt in range(T):
                            last = nc.tensor.transpose(bank(6)[:, kt * S + qt * P:kt * S + qt * P + P],
                                                       xp[:, qt, kt * P:(kt + 1) * P], ident[:])
                    last.then_inc(p_tr, 1)
                if project:
                    pe.wait_ge(xnT_done, b + 1)
                    wait(pe, qT_x, KC * b)
                    project_T(wq_sb, xnT, 3, q_mm)
                if finish:
                    pe.wait_ge(pT_x, b)
                    pe.wait_ge(v_x, b)
                    wait(pe, xc_done, T * (b - 1))
                    for qt in range(T):
                        for kt in range(T):
                            last = mm(bank(7)[:, qt * D:(qt + 1) * D], xpT[:, kt, qt * P:(qt + 1) * P],
                                      xv[:, kt, :], start=(kt == 0), stop=(kt == T - 1))
                    last.then_inc(ctx_mm, 1)
                if project:
                    pe.wait_ge(kT_x, KC * (b + 1))
                    pe.wait_ge(qT_x, KC * (b + 1))
                    wait(pe, smax, T * b)
                    for qt in range(T):
                        for k in range(KC):
                            last = mm(bank(5)[:, qt * S:(qt + 1) * S], xqT[:, k, qt * P:(qt + 1) * P],
                                      xkT[:, k, :], start=(k == 0), stop=(k == KC - 1))
                    last.then_inc(s_mm, 1)

            run_x(pe, turn)

            pe.wait_ge(zeros_set, ZEROS)
            pe.wait_ge(ynext_in, 16)
            transpose_rows(y_next, 0).then_inc(y_tr, 1)

            def bias_products(l):
                pe.wait_ge(wb_in, 48 * (l + 1))
                wait(pe, res_done, NB * l)
                for c in range(HC):
                    for half in range(2):
                        o = half * HID + c * P
                        for k in range(KC):
                            last = mm(ps[0:hrows[c], 7, half * HC + c:half * HC + c + 1],
                                      w1_raw[:, k, o:o + hrows[c]], lgb[:, l, 1, k:k + 1],
                                      start=(k == 0), stop=(k == KC - 1))
                last.then_inc(b1_mm, 1)

            def step(s, la, lf):
                f = s - 1

                def project(t, parts):
                    i = 0 if t == 0 else 3
                    if t == 0 and 0 in parts:
                        pe.wait_ge(yT_done, s + 1)
                    elif 0 in parts:
                        wait(pe, pT_done, HEADS * s)
                    for j in parts:
                        if j == 2:
                            if t == 0:
                                wait(pe, x1_done, s)
                            else:
                                pe.wait_ge(v_done, T * s + t)
                        if t == 0 and isinstance(s, int) and s in (0, NB):
                            pe.wait_ge(w_ready, PIECES * la + j + 1)
                        o = bank(i + j) if j < 2 else bank(2)
                        for k in range(KC):
                            c0 = k * YTC - k + t * P
                            last = split_product(o, lambda a: yT[a][:, c0:c0 + P],
                                                 lambda a: wqkv_hl[a][:, k, j * INNER:(j + 1) * INNER],
                                                 k == 0, k == KC - 1)
                        if j:
                            last.then_inc((None, qk_mm, v_mm2)[j], 1)

                def up(c):
                    i, r = 5 + c % 2, hrows[c]
                    if c == 0:
                        pe.wait_ge(hT_done, s)
                        if lf == 1 or (isinstance(s, int) and s == 1):
                            pe.wait_ge(w_ready, PIECES * (lf + 1))
                    if c < 2:
                        pe.wait_ge(o_done, PAIRS * s)
                    else:
                        pe.wait_ge(u_raw, HC * f + c - 1)
                    for half in range(2):
                        o = half * HID + c * P
                        for k in range(KC):
                            last = split_product(ps[0:r, i, half * S:(half + 1) * S],
                                                 lambda a: w1_hl[a][:, k, o:o + r], lambda a: hT[a][:, k, :],
                                                 k == 0, k == KC - 1)
                    last.then_inc(up_mm, 1)

                def tr_heads(t):
                    i = 0 if t == 0 else 3
                    pe.wait_ge(sq_done, T * s + t + 1)
                    for j in range(2):
                        pe.wait_ge((sum_done, ks_done)[j], T * s + t + 1)
                        for c in range(PAIRS):
                            last = nc.tensor.transpose(bank(i + j)[:, c * P:(c + 1) * P],
                                                       t1[:, t, j * INNER + c * P:j * INNER + (c + 1) * P],
                                                       ident[:])
                        last.then_inc(qk_tr, 1)

                def scores(h):
                    b = bank(h % NS)
                    if h >= NS:
                        pe.wait_ge(mx_done, T * (HEADS * s + h - NS + 1))
                    mm(b[:, 0:P], qz[:, h, 0:P], kT[:, h // 2, 0:P], start=True, stop=True)
                    mm(b[:, P:3 * P], qz[:, h, P:S], kT[:, h // 2, :], start=True, stop=True)\
                        .then_inc(s_mm2, 1)

                def tr_probs(h):
                    b, p = bank(3 + h % 2), pr[:, h % NS, :]
                    pe.wait_ge(pn_done, T * (HEADS * s + h + 1))
                    if h >= 2:
                        pe.wait_ge(pT_done, HEADS * s + h - 1)
                    nc.tensor.transpose(b[:, 0:P], p[:, 2 * P:3 * P], ident[:])
                    nc.tensor.transpose(b[:, P:2 * P], p[:, 0:P], ident[:])
                    nc.tensor.transpose(b[:, 2 * P:3 * P], p[:, P:2 * P], ident[:]).then_inc(pt_tr, 1)

                def weighted(h):
                    pair, j = h // 2, h % 2
                    b = bank(5 + pair % 2)
                    pe.wait_ge(pT_done, HEADS * s + h + 1)
                    if j == 0:
                        if pair < 2:
                            if lf is not None:
                                pe.wait_ge(u_done, HC * s)
                        else:
                            pe.wait_ge(o_done, PAIRS * s + pair - 1)
                    v = [vz[:, t, pair, j:j + 2, :].rearrange("p a d -> p (a d)") for t in range(T)]
                    mm(b[:, 0:S], v[0], pT[:, h % 2, P:3 * P], start=(j == 0), stop=False)
                    mm(b[:, P:S], v[1], pT[:, h % 2, 0:P], start=False, stop=(j == 1)).then_inc(pv_mm, 1)

                def down(n):
                    t, c = n // HC, n % HC
                    if n == 0:
                        pe.wait_ge(u_done, HC * s)
                    last = split_product(bank(7)[:, t * D:(t + 1) * D], lambda a: u[a][:, c, t * P:(t + 1) * P],
                                         lambda a: w2_hl[a][:, c, :], c == 0, c == HC - 1)
                    if n == T * HC - 1:
                        last.then_inc(dn_mm, 1)

                def shift_rows():
                    pe.wait_ge(x1_done, s)
                    wait(pe, res_done, f)
                    if lf == 1 or (isinstance(s, int) and s == 1):
                        pe.wait_ge(b1_done, 2 * (lf + 1))
                    o = bank(7)[:, 0:T * P].rearrange("p (t n) -> p t n", t=T)
                    mm(o[:, 0, :], shift[:, 0:P], x1[:, 0, P:D], start=True, stop=True)
                    mm(o[:, 1, :], shift[:, 0:P], x1[:, 1, P:D], start=True, stop=False)
                    mm(o[:, 1, :], shift[:, P:2 * P], x1[:, 0, P:D], start=False, stop=True).then_inc(sh_mm, 1)

                A, F = la is not None, lf is not None
                if A:
                    project(0, (0, 1))
                if F:
                    shift_rows()
                if A:
                    project(0, (2,))
                    project(1, (0, 1))
                if F:
                    pe.wait_ge(hn_done, s)
                    transpose_rows(hn, 7).then_inc(h_tr, 1)
                if A:
                    project(1, (2,))
                if F:
                    up(0)
                    up(1)
                if A:
                    tr_heads(0)
                if F:
                    up(2)
                    up(3)
                if A:
                    tr_heads(1)
                if F:
                    for c in range(4, HC):
                        up(c)
                if A:
                    pe.wait_ge(q_done, 2 * T * (s + 1))
                    pe.wait_ge(k_done, T * (s + 1))
                    pe.wait_ge(v_done, T * (s + 1))
                    for h in range(NS):
                        scores(h)
                n = 0
                if A:
                    for h in range(HEADS + 1):
                        if h + NS < HEADS:
                            scores(h + NS)
                        if h < HEADS:
                            tr_probs(h)
                        if F:
                            while n * (HEADS + 2) < T * HC * (h + 1):
                                down(n)
                                n += 1
                        if h:
                            weighted(h - 1)
                    if not (isinstance(s, int) and s == STEPS - 1):
                        pe.wait_ge(ynext_in, 16 * (s + 2))
                        pe.wait_ge(mx_done, T * HEADS * (s + 1))
                        transpose_rows(y_next, 0).then_inc(y_tr, 1)
                if F:
                    while n < T * HC:
                        down(n)
                        n += 1
                if A:
                    pe.wait_ge(o_done, PAIRS * (s + 1))
                    if isinstance(s, int) and s in (0, NB):
                        pe.wait_ge(w_ready, PIECES * la + FIRST)
                    for t in range(T):
                        for c in range(PAIRS):
                            last = split_product(bank(2)[:, t * D:(t + 1) * D],
                                                 lambda a: oT[a][:, c, t * P:(t + 1) * P],
                                                 lambda a: wo_hl[a][:, c, :], c == 0, c == PAIRS - 1)
                    last.then_inc(wo_mm, 1)
                if isinstance(s, int) and s in (0, NB):
                    bias_products(la)

            run_steps(pe, step)

        @block.scalar
        def _(act):
            A = nc.scalar.activation
            act.wait_ge(cst_in, 16 * 7)
            A(tg[:], g_in[:], ACT.Tanh).then_inc(tanh_done, 1)

            def high_parts(l, first):
                act.wait_ge(wa_in if first else wb_in, 16 * (2 if first else 3) * (l + 1))
                if l:
                    act.wait_ge(wo_mm if first else dn_mm, NB)
                if not first:
                    act.wait_ge(w1_scaled, KC * (l + 1))
                for full, high, low in pieces(l, first):
                    A(high, full, ACT.Copy).then_inc(w_high, 1)

            def turn(b, project, finish, ahead):
                def projected(i):
                    mm_done, done, dst, j = ((k_mm, kT_x, xkT, 1), (q_mm, qT_x, xqT, 0))[i]
                    act.wait_ge(mm_done, b + 1)
                    wait(act, s_mm, b)
                    for m in range(KC):
                        A(dst[:, m, :], halves(2 + i)[:, m, :], ACT.Identity,
                          bias=bqk[:, j, m:m + 1]).then_inc(done, 1)

                if project:
                    act.wait_ge(c_tr, b + 1)
                    wait(act, v_mm, b)
                    A(cT, halves(0), ACT.Copy).then_inc(cT_done, 1)
                    act.wait_ge(xn_tr, b + 1)
                    wait(act, q_mm, b)
                    A(xnT, halves(1), ACT.Copy).then_inc(xnT_done, 1)
                    projected(0)
                if finish:
                    act.wait_ge(p_tr, b)
                    wait(act, ctx_mm, b - 1)
                    A(xpT, halves(6), ACT.Copy).then_inc(pT_x, 1)
                if project:
                    projected(1)
                    act.wait_ge(nbx, b + 1)
                    wait(act, rlx, b)
                    for t in range(T):
                        A(xp[:, t, :], xs[:, t, :], ACT.Exp, bias=xnb[:, t:t + 1], scale=XSCALE,
                          accum_out=xl[:, t:t + 1]).then_inc(exp_x, 1)

            run_x(act, turn, lambda: high_parts(0, True))

            def evac_yT(n):
                act.wait_ge(y_tr, n)
                dst = yT[0][:].rearrange("p (k c) -> p k c", c=YTC)[:, :, 0:S]
                A(dst, halves(0), ACT.Copy).then_inc(yT_high, 1)

            act.wait_ge(zeros_set, ZEROS)
            evac_yT(1)

            def step(s, la, lf):
                f = s - 1

                def squares(t):
                    act.wait_ge(qk_mm, T * s + t + 1)
                    wait(act, ss_done, T * s + t)
                    i = 0 if t == 0 else 3
                    A(sqb[:].rearrange("p (a n) -> p a n", a=2), ps[:, i:i + 2, :], ACT.Square)\
                        .then_inc(sq_done, 1)

                def values(t):
                    act.wait_ge(v_mm2, T * s + t + 1)
                    wait(act, pv_mm, HEADS * s)
                    A(vz[:, t, :, 0:3:2, :], bank(2).rearrange("p (a j d) -> p a j d", a=PAIRS, j=2),
                      ACT.Copy).then_inc(v_done, 1)

                def gelu(c):
                    act.wait_ge(up_mm, HC * f + c + 1)
                    wait(act, u_raw, HC * f + max(0, c - 1))
                    r = hrows[c]
                    A(gl[0:r, c % 2, :], ps[0:r, 5 + c % 2, S:2 * S], ACT.Gelu,
                      bias=b1_sb[0:r, lf, 1, c:c + 1]).then_inc(gl_done, 1)

                def heads_T(t):
                    i = 0 if t == 0 else 3
                    act.wait_ge(qk_tr, 2 * (T * s + t) + 1)
                    wait(act, s_mm2, HEADS * s)
                    q = qz[:].rearrange("p (c j) n -> p c j n", j=2)
                    for j in range(2):
                        lo = j * DH
                        A(q[lo:lo + DH, :, j, t * P:(t + 1) * P],
                          ps[lo:lo + DH, i, :].rearrange("p (c n) -> p c n", c=PAIRS), ACT.Copy)\
                            .then_inc(q_done, 1)
                    act.wait_ge(qk_tr, 2 * (T * s + t) + 2)
                    A(kT[:, :, t * P:(t + 1) * P], bank(i + 1).rearrange("p (c n) -> p c n", c=PAIRS),
                      ACT.Copy).then_inc(k_done, 1)

                def exps(h):
                    act.wait_ge(nb_done, HEADS * s + h + 1)
                    if h >= NS:
                        act.wait_ge(pt_tr, HEADS * s + h - NS + 1)
                    wait(act, rl_done, HEADS * s)
                    for t, (a, b) in enumerate(((0, P), (P, 3 * P))):
                        A(pr[:, h % NS, a:b], sm[:, h % NS, a:b], ACT.Exp, bias=nb[:, h, t:t + 1],
                          scale=rn8[:, t, h:h + 1], accum_out=ls[:, h, t:t + 1]).then_inc(e_done, 1)

                def probs_T(h):
                    act.wait_ge(pt_tr, HEADS * s + h + 1)
                    wait(act, pv_mm, HEADS * s + h - 1)
                    A(pT[:, h % 2, :], bank(3 + h % 2)[:, 0:3 * P], ACT.Copy).then_inc(pT_done, 1)

                def heads_out(pair):
                    act.wait_ge(pv_mm, HEADS * s + 2 * pair + 2)
                    wait(act, wo_mm, s)
                    A(oT[0][:, pair, :], bank(5 + pair % 2)[:, 0:S], ACT.Copy).then_inc(o_high, 1)

                if isinstance(s, int) and s == NB:
                    high_parts(1, True)
                if la is not None:
                    squares(0)
                    values(0)
                if lf is not None:
                    act.wait_ge(h_tr, s)
                    wait(act, up_mm, HC * f)
                    A(hT[0][:], halves(7), ACT.Copy).then_inc(hT_high, 1)
                if la is not None:
                    squares(1)
                    values(1)
                if lf is not None:
                    gelu(0)
                    gelu(1)
                if la is not None:
                    heads_T(0)
                if lf is not None:
                    gelu(2)
                    gelu(3)
                if la is not None:
                    heads_T(1)
                if lf is not None:
                    for c in range(4, HC):
                        gelu(c)
                if la is not None:
                    exps(0)
                    exps(1)
                    for h in range(HEADS):
                        if h + 2 < HEADS:
                            exps(h + 2)
                        if h >= 3 and h % 2:
                            heads_out((h - 3) // 2)
                        probs_T(h)
                    heads_out(PAIRS - 1)
                    if not (isinstance(s, int) and s == STEPS - 1):
                        evac_yT(s + 2)
                if isinstance(s, int) and s in (0, NB):
                    high_parts(la, False)

            run_steps(act, step)

        @block.vector
        def _(dve):
            V = nc.vector
            for part in yT:
                V.memset(part[:].bitcast(F32), 0.0).then_inc(zeros_set, 1)
            V.memset(qz[:], 0.0).then_inc(zeros_set, 1)
            V.memset(vz[:], 0.0).then_inc(zeros_set, 1)
            for part in u:
                V.memset(part[:].bitcast(F32), 0.0).then_inc(zeros_set, 1)
            V.memset(nhalf[:], -0.5).then_inc(zeros_set, 1)
            for part in w2_hl:
                V.memset(part[:, HC - 1, :].bitcast(F32), 0.0).then_inc(zeros_set, 1)

            def statistics(kind, n, values):
                for t in range(T):
                    V.bn_stats(xst[:, kind, t, :], values[:, t, :]).then_inc(stats[kind], 1)
                for t in range(T):
                    wait_apart(dve, dve_passed, (stats[kind], T * n + t + 1))
                    V.bn_aggr(xmv[:, kind, t, :], xst[:, kind, t, :]).then_inc(var[kind], 1)

            def normalised(kind, n, dst, src, done):
                dve.wait_ge(rstd_done[kind], n + 1)
                for t in range(T):
                    V.tensor_scalar(dst[:, t, :], src[:, t, :], xmv[:, kind, t, 0:1], xrs[:, kind, t:t + 1],
                                    ALU.subtract, ALU.mult).then_inc(done, 1)

            def turn(b, project, finish, ahead):
                if project:
                    dve.wait_ge(m_loaded, 16 * (b + 1))
                    wait(dve, smax, T * b)
                    V.tensor_scalar(mbias, m_in, 0, NEG, ALU.is_equal, ALU.mult).then_inc(mb_done, 1)
                if finish:
                    dve.wait_ge(ctx_mm, b)
                    dve.wait_ge(rlx, b)
                    wait(dve, tg_done, b - 1)
                    for t in range(T):
                        V.tensor_scalar(xc[:, t, :], halves(7)[:, t, :], xrl[:, t:t + 1], None,
                                        ALU.mult).then_inc(xc_done, 1)
                    dve.wait_ge(xc_done, T * b)
                    statistics(1, b - 1, xc)
                if project:
                    dve.wait_ge(v_mm, b + 1)
                    V.tensor_tensor(xv, halves(4), bv_bc[:].unsqueeze(1).to_broadcast([P, T, D]),
                                    ALU.add).then_inc(v_x, 1)
                if ahead:
                    dve.wait_ge(x_loaded, 16 * (b + 2))
                    statistics(0, b + 1, x_in)
                if finish:
                    normalised(1, b - 1, xc, xc, tn_done)
                    dve.wait_ge(tn_done, T * b)
                    V.tensor_tensor(xc, xc, gam_bc[:].unsqueeze(1).to_broadcast([P, T, D]),
                                    ALU.mult).then_inc(tg_done, 1)
                    dve.wait_ge(tg_done, b)
                    dve.wait_ge(xrb_done, b)
                    wait(dve, xmid_stored, 16 * (b - 1))
                    V.tensor_tensor(x_mid, xc, x_res, ALU.add).then_inc(xmid_done, 1)
                    dve.wait_ge(xmid_done, b)
                    statistics(2, b - 1, x_mid)
                if ahead:
                    dve.wait_ge(xn_tr, b + 1)
                    normalised(0, b + 1, xn, x_in, xn_done)
                if project:
                    wait_apart(dve, dve_passed, (s_mm, b + 1),
                                               (mb_done, b + 1),
                                               (exp_x, T * b))
                    for t in range(T):
                        V.tensor_tensor_reduce(xs[:, t, :], halves(5)[:, t, :], mbias[:, t, :], 1.0, NEG,
                                               ALU.add, ALU.max, xmx[:, t:t + 1]).then_inc(smax, 1)
                    dve.wait_ge(smax, T * (b + 1))
                    V.tensor_scalar(xnb[:], xmx[:], -XSCALE, None, ALU.mult).then_inc(nbx, 1)
                if finish:
                    wait(dve, y_stored, 16 * (b - 1))
                    normalised(2, b - 1, y_new, x_mid, y_done_x)
                if project:
                    dve.wait_ge(exp_x, T * (b + 1))
                    wait(dve, xc_done, T * b)
                    V.reciprocal(xrl[:], xl[:]).then_inc(rlx, 1)

            def low_parts(l, first):
                for i, (full, high, low) in enumerate(pieces(l, first)):
                    dve.wait_ge(w_high, PIECES * l + (0 if first else FIRST) + i + 1)
                    V.tensor_tensor(low, full, high.bitcast(F32), ALU.subtract).then_inc(w_ready, 1)

            def fold_affine(l):
                dve.wait_ge(b1_mm, l + 1)
                sums = ps[:, 7, 0:2 * HC].rearrange("p (h c) -> p h c", h=2)
                for r, c in ((P, slice(0, HC - 1)), (HT, slice(HC - 1, HC))):
                    V.tensor_tensor(b1_sb[0:r, l, :, c], b1_sb[0:r, l, :, c], sums[0:r, :, c],
                                    ALU.add).then_inc(b1_done, 1)
                for k in range(KC):
                    V.tensor_scalar(w1_raw[:, k, :], w1_raw[:, k, :], lgb[:, l, 0, k:k + 1], None,
                                    ALU.mult).then_inc(w1_scaled, 1)
                dve.wait_ge(b1_done, 2 * (l + 1))
                dve.wait_ge(w1_scaled, KC * (l + 1))

            def low_yT(n):
                dve.wait_ge(yT_high, n)
                hi, lo = (p[:].rearrange("p (k c) -> p k c", c=YTC)[:, :, 0:S] for p in yT)
                V.tensor_tensor(lo, halves(0), hi.bitcast(F32), ALU.subtract).then_inc(yT_done, 1)

            dve.wait_ge(x_loaded, 16)
            statistics(0, 0, x_in)
            normalised(0, 0, xn, x_in, xn_done)
            dve.wait_ge(cst_in, 16 * 7)
            dve.wait_ge(tanh_done, 1)
            V.tensor_scalar(gam_bc[:], gam_bc[:], tg[:, 0:1], None, ALU.mult).then_inc(prep_done, 1)
            V.tensor_scalar(bet_bc[:], bet_bc[:], tg[:, 0:1], None, ALU.mult).then_inc(prep_done, 1)
            dve.wait_ge(prep_done, 2)
            run_x(dve, turn, lambda: low_parts(0, True))

            dve.wait_ge(cst2_in, CONSTS)
            H = DH // 2
            for l in range(DEPTH):
                sc = qks[:, l, :].rearrange("p (a d) -> p a d", a=2).unsqueeze(1).to_broadcast([P, T, 2, DH])
                cos, sin = (rtab[:, :, i, :].rearrange("p t (a d) -> p t a d", a=2) for i in range(2))
                V.tensor_tensor(tc_sb[l][:], cos, sc, ALU.mult).then_inc(prep_done, 1)
                V.tensor_tensor(ts_sb[l][:, :, :, 0:H], sin[:, :, :, 0:H], sc[:, :, :, H:DH],
                                ALU.mult).then_inc(prep_done, 1)
                V.tensor_tensor(ts_sb[l][:, :, :, H:DH], sin[:, :, :, H:DH], sc[:, :, :, 0:H],
                                ALU.mult).then_inc(prep_done, 1)
            dve.wait_ge(prep_done, 2 + 3 * DEPTH)
            dve.wait_ge(zeros_set, ZEROS)
            low_yT(1)

            def step(s, la, lf):
                f = s - 1

                def norms(t):
                    dve.wait_ge(sq_done, T * s + t + 1)
                    wait(dve, rn_done, T * (s - 1) + t + 1 if not isinstance(s, int) or s else 0)
                    V.tensor_reduce(ss[:, t, :], sqb[:].rearrange("p (h d) -> p h d", d=DH), AX.X,
                                    ALU.add).then_inc(ss_done, 1)

                def rotate(t):
                    i = 0 if t == 0 else 3
                    wait(dve, qk_tr, 2 * (T * (s - 1) + t + 1) if not isinstance(s, int) or s else 0)
                    wait(dve, sum_done, T * s + t)
                    qk = ps[:, i:i + 2, :].rearrange("p a (h d) -> p a h d", d=DH)
                    a1, a2 = (b.rearrange("p (a h d) -> p a h d", a=2, d=DH) for b in (t1[:, t, :], t2))
                    tc = tc_sb[la][:, t].unsqueeze(2).to_broadcast([P, 2, HEADS, DH])
                    ts = ts_sb[la][:, t].unsqueeze(2).to_broadcast([P, 2, HEADS, DH])
                    V.tensor_tensor(a1, qk, tc, ALU.mult)
                    V.tensor_tensor(a2[:, :, :, 0:H], qk[:, :, :, H:DH], ts[:, :, :, 0:H], ALU.mult)
                    V.tensor_tensor(a2[:, :, :, H:DH], qk[:, :, :, 0:H], ts[:, :, :, H:DH], ALU.mult)\
                        .then_inc(rot_done, 1)

                def add_rotated(t):
                    dve.wait_ge(rot_done, T * s + t + 1)
                    V.tensor_tensor(t1[:, t, :], t1[:, t, :], t2, ALU.add).then_inc(sum_done, 1)

                def scale_keys(t):
                    dve.wait_ge(sum_done, T * s + t + 1)
                    dve.wait_ge(rn_done, T * s + t + 1)
                    kh = t1[:, t, INNER:2 * INNER].rearrange("p (h d) -> p h d", d=DH)
                    rk = rn[:, t, HEADS:2 * HEADS].unsqueeze(2).to_broadcast([P, HEADS, DH])
                    V.tensor_tensor(kh, kh, rk, ALU.mult).then_inc(ks_done, 1)

                def low_hT():
                    dve.wait_ge(hT_high, s)
                    V.tensor_tensor(hT[1][:], halves(7), hT[0][:].bitcast(F32), ALU.subtract).then_inc(hT_done, 1)

                def gated(c):
                    dve.wait_ge(gl_done, HC * f + c + 1)
                    wait(dve, dn_mm, f)
                    wait(dve, u_done, HC * f + c - 1)
                    r = hrows[c]
                    full = u_full[0:r, c % 2, :]
                    V.scalar_tensor_tensor(full, ps[0:r, 5 + c % 2, 0:S], b1_sb[0:r, lf, 0, c:c + 1],
                                           gl[0:r, c % 2, :], ALU.add, ALU.mult).then_inc(u_raw, 1)
                    dve.wait_ge(u_raw, HC * f + c + 1)
                    V.tensor_copy(u[0][0:r, c, :], full).then_inc(u_high, 1)

                def low_oT(pair):
                    dve.wait_ge(o_high, PAIRS * s + pair + 1)
                    V.tensor_tensor(oT[1][:, pair, :], bank(5 + pair % 2)[:, 0:S],
                                    oT[0][:, pair, :].bitcast(F32), ALU.subtract).then_inc(o_done, 1)

                def row_max(h):
                    wait_apart(dve, dve_passed, (s_mm2, HEADS * s + h + 1),
                               (e_done, T * (HEADS * s + max(0, h - NS + 1))),
                               (nb_done, HEADS * s))
                    for t, (a, b) in enumerate(((0, P), (P, 3 * P))):
                        V.tensor_tensor_reduce(sm[:, h % NS, a:b], bank(h % NS)[:, a:b], wmask[:, a:b], 1.0,
                                               NEG, ALU.add, ALU.max, mx[:, h, t:t + 1]).then_inc(mx_done, 1)
                    dve.wait_ge(mx_done, T * (HEADS * s + h + 1))
                    dve.wait_ge(rn8_done, 2 * T * (s + 1))
                    V.tensor_tensor(nb[:, h, :], mx[:, h, :], nrn8[:, :, h], ALU.mult).then_inc(nb_done, 1)

                def row_sum(h):
                    dve.wait_ge(e_done, T * (HEADS * s + h + 1))
                    wait(dve, pn_done, T * HEADS * s)
                    V.reciprocal(rl[:, h, :], ls[:, h, :]).then_inc(rl_done, 1)

                A, F = la is not None, lf is not None

                def shifted_halves(t):
                    return (x1[:, t, 0:P], bank(7)[:, t * P:(t + 1) * P])

                def row_statistics():
                    dve.wait_ge(sh_mm, s)
                    for t in range(T):
                        for i, half in enumerate(shifted_halves(t)):
                            V.bn_stats(hst[:, t, i, :], half).then_inc(hbn_a, 1)
                    wait(dve, heps, f)
                    for t in range(T):
                        wait_apart(dve, dve_passed, (hbn_a, 2 * (T * f + t + 1)))
                        V.bn_aggr(hmv[:, t, :], hst[:, t, :, :]).then_inc(hbn, 1)

                def normalise_rows():
                    dve.wait_ge(hrstd, s)
                    wait(dve, h_tr, f)
                    for t in range(T):
                        for i, half in enumerate(shifted_halves(t)):
                            last = V.tensor_scalar(hn[:, t, i * P:(i + 1) * P], half, hmv[:, t, 0:1],
                                                   hrs[:, t:t + 1], ALU.subtract, ALU.mult)
                    last.then_inc(hn_done, 1)

                if isinstance(s, int) and s == NB:
                    low_parts(1, True)
                if F:
                    row_statistics()
                if A:
                    norms(0)
                if F:
                    normalise_rows()
                if A:
                    rotate(0)
                if F:
                    low_hT()
                if A:
                    add_rotated(0)
                    norms(1)
                    scale_keys(0)
                if F:
                    gated(0)
                if A:
                    rotate(1)
                if F:
                    gated(1)
                if A:
                    add_rotated(1)
                    scale_keys(1)
                if F:
                    for c in range(2, HC):
                        gated(c)
                if A:
                    for h in range(NS):
                        row_max(h)
                    row_sum(0)
                    for h in range(HEADS):
                        if h + 1 < HEADS:
                            row_sum(h + 1)
                        if h + NS < HEADS:
                            row_max(h + NS)
                        if h >= 4 and h % 2 == 0:
                            low_oT((h - 4) // 2)
                    low_oT(PAIRS - 2)
                    low_oT(PAIRS - 1)
                    if not (isinstance(s, int) and s == STEPS - 1):
                        low_yT(s + 2)
                if F:
                    dve.wait_ge(dn_mm, s)
                    dve.wait_ge(xb_done, s)
                    wait(dve, res_stored, 16 * f)
                    V.tensor_tensor(yo, halves(7), x1b, ALU.add).then_inc(yo_done if lf else res_done, 1)
                    if lf == 1:
                        dve.wait_ge(yo_done, s - NB)
                        dve.wait_ge(xm_in, 16 * (s - NB))
                        V.scalar_tensor_tensor(yo, yo, tg[:, 1:2], xm_res,
                                               ALU.mult, ALU.add).then_inc(res_done, 1)
                if A:
                    dve.wait_ge(wo_mm, s + 1)
                    dve.wait_ge(yres_in, 16 * (s + 1))
                    wait(dve, hn_done, s)
                    wait(dve, xb_done, s)
                    V.tensor_tensor(x1[:], halves(2), y_res[:], ALU.add).then_inc(x1_done, 1)
                if isinstance(s, int) and s in (0, NB):
                    fold_affine(la)
                    low_parts(la, False)

            run_steps(dve, step)

        @block.gpsimd
        def _(pool):
            G = nc.gpsimd
            pool.wait_ge(zeros_set, ZEROS)

            def rstd(var, dst, a, b, after_a):
                G.tensor_scalar(dst, var, LN_EPS, 1.0, ALU.add, ALU.mult).then_inc(a, 1)
                pool.wait_ge(a, after_a)
                G.tensor_tensor(dst, dst, nhalf[:, 0:T], ALU.pow).then_inc(b, 1)

            def rstd_x(kind, n):
                wait_apart(pool, pool_passed, (var[kind], T * (n + 1)))
                rstd(xmv[:, kind, :, 1], xrs[:, kind, :], eps_add[kind], rstd_done[kind], n + 1)

            def turn(b, project, finish, ahead):
                if finish:
                    rstd_x(1, b - 1)
                if ahead:
                    rstd_x(0, b + 1)
                if finish:
                    pool.wait_ge(xres_loaded, 16 * b)
                    G.tensor_tensor(x_res, x_res, bet_bc[:].unsqueeze(1).to_broadcast([P, T, D]),
                                    ALU.add).then_inc(xrb_done, 1)
                    rstd_x(2, b - 1)

            rstd_x(0, 0)
            pool.wait_ge(prep_done, 2)
            run_x(pool, turn)
            pool.wait_ge(cst2_in, CONSTS)

            def step(s, la, lf):
                f = s - 1

                def inverse_norms(t):
                    wait_apart(pool, pool_passed, (ss_done, T * s + t + 1))
                    G.tensor_scalar(ss[:, t, :], ss[:, t, :], L2_EPS2, 1.0, ALU.max, ALU.mult)\
                        .then_inc(ssc_done, 1)
                    pool.wait_ge(ssc_done, T * s + t + 1)
                    wait(pool, e_done, T * HEADS * s)
                    G.tensor_tensor(rn[:, t, :], ss[:, t, :], nhalf[:], ALU.pow).then_inc(rn_done, 1)
                    wait_apart(pool, pool_passed, (rn_done, T * s + t + 1))
                    G.tensor_scalar(rn8[:, t, :], rn[:, t, 0:HEADS], QK_SCALE, 1.0, ALU.mult, ALU.mult)\
                        .then_inc(rn8_done, 1)
                    G.tensor_scalar(nrn8[:, t, :], rn[:, t, 0:HEADS], -QK_SCALE, 1.0, ALU.mult, ALU.mult)\
                        .then_inc(rn8_done, 1)

                def low_u(c):
                    pool.wait_ge(u_high, HC * f + c + 1)
                    r = hrows[c]
                    G.tensor_tensor(u[1][0:r, c, :], u_full[0:r, c % 2, :], u[0][0:r, c, :].bitcast(F32),
                                    ALU.subtract).then_inc(u_done, 1)

                def normalise(h):
                    wait_apart(pool, pool_passed, (rl_done, HEADS * s + h + 1))
                    for t, (a, b) in enumerate(((0, P), (P, 3 * P))):
                        G.tensor_scalar(pr[:, h % NS, a:b], pr[:, h % NS, a:b], rl[:, h, t:t + 1], 1.0,
                                        ALU.mult, ALU.mult).then_inc(pn_done, 1)

                if lf is not None:
                    wait_apart(pool, pool_passed, (hbn, T * s),
                                                (hn_done, f))
                    rstd(hmv[:, :, 1], hrs[:], heps, hrstd, s)
                if la is not None:
                    inverse_norms(0)
                if lf is not None:
                    pool.wait_ge(x1_done, s)
                    wait(pool, res_done, f)
                    G.tensor_tensor(x1b, x1[:], b2_bc[lf][:].unsqueeze(1).to_broadcast([P, T, D]),
                                    ALU.add).then_inc(xb_done, 1)
                if la is not None:
                    inverse_norms(1)
                if lf is not None:
                    for c in range(HC):
                        low_u(c)
                if la is not None:
                    for h in range(HEADS):
                        normalise(h)

            run_steps(pool, step)


CONSTS = 16 * 21
ZEROS = 7 + 2


def host_tables(S):
    import numpy as np
    half = np.arange(0, DH, 2, dtype=np.float32)
    inv = (np.float32(1.0) / np.float32(10000.0) ** (half / np.float32(DH))).astype(np.float32)
    t = np.arange(S, dtype=np.float32)
    fr = t[:, None] * inv[None, :]
    base = (half + np.float32(0.4 * DH)) / np.float32(1.4 * DH)
    power = (t - S // 2) / np.float32(64)
    sc = base[None, :].astype(np.float64) ** power[:, None].astype(np.float64)
    cos, sin = np.cos(fr.astype(np.float64)), np.sin(fr.astype(np.float64))

    def both(a, b):
        return np.concatenate([a, b], axis=1)
    tab = np.stack([both(both(cos * sc, cos * sc), both(cos / sc, cos / sc)),
                    both(both(-sin * sc, sin * sc), both(-sin / sc, sin / sc))], axis=1)
    tab = tab.reshape(S // P, P, 2, 2 * DH).transpose(1, 0, 2, 3)
    i, j = np.arange(P)[:, None], np.arange(P)[None, :]
    own, prev = np.where(j <= i, 0.0, NEG), np.where(j >= i, 0.0, NEG)
    return (np.ascontiguousarray(tab, np.float32),
            np.concatenate([own, prev, own], axis=1).astype(np.float32), np.eye(P, dtype=np.float32),
            np.eye(P, 2 * P, 1, dtype=np.float32))


_INS = ['x', 'ctx_1024', 'mask_BxSxS2_ik1', 'g_xattn', 'g_ffn', 'L0_xattn_Wq', 'L0_xattn_bq', 'L0_xattn_Wk',
        'L0_xattn_bk', 'L0_xattn_Wv', 'L0_xattn_bv', 'L0_xattn_ln_gamma', 'L0_xattn_ln_beta', 'L0_ffn_wqkv',
        'L0_ffn_q_scale', 'L0_ffn_k_scale', 'L0_ffn_wo', 'L0_ffn_ln_g', 'L0_ffn_ln_b', 'L0_ffn_w1',
        'L0_ffn_b1', 'L0_ffn_w2', 'L0_ffn_b2']


def kernel(**inputs):
    import numpy as np
    import concourse.bacc as bacc
    from concourse.bass_utils import run_bass_kernel_spmd

    arrays = {n: np.ascontiguousarray(inputs[n]) for n in _INS}
    tab, win, eye, down = host_tables(arrays['x'].shape[1])
    arrays.update(rot_tab=tab, win_mask=win, identity=eye, row_shift=down)
    nc = bacc.Bacc("TRN2", target_bir_lowering=False, num_devices=1)
    args = [nc.dram_tensor(n, a.shape, mybir.dt.from_np(a.dtype), kind="ExternalInput").ap()
            for n, a in arrays.items()]
    out = nc.dram_tensor("out", arrays['x'].shape, F32, kind="ExternalOutput").ap()
    build(nc, *args, out)
    r = run_bass_kernel_spmd(nc, [arrays], core_ids=[0])
    return r.results[0]["out"]
```

```python
from contextlib import ExitStack

import concourse.bass as bass
from concourse import mybir

P = 128
F32 = mybir.dt.float32
F32R = mybir.dt.float32r
I32 = mybir.dt.int32
ALU = mybir.AluOpType
ACT = mybir.ActivationFunctionType
AX = mybir.AxisListType

NEG = -1.0e30
LN_EPS = 1e-5
L2_EPS2 = 1e-24
HEADS, DH = 8, 64
QK_SCALE = 8.0


def wait(eng, semaphore, value):
    if isinstance(value, int) and value <= 0:
        return
    eng.wait_ge(semaphore, value)


def wait_apart(eng, passed, *waits):
    for semaphore, value in waits:
        wait(eng, semaphore, value)
    eng.sem_inc(passed, 1)


def build(nc, x, ctx_in, mask, g_xattn, g_ffn, Wq, bq, Wk, bk, Wv, bv, ln_gamma, ln_beta,
          wqkv, q_scale, k_scale, wo, ln_g, ln_b, w1, b1, w2, b2, rot_tab, win_mask, ident_in, shift_in, out):
    NB, S, D = x.shape
    T = S // P
    KC = D // P
    DEPTH = wqkv.shape[0]
    INNER = HEADS * DH
    PAIRS = HEADS // 2
    HID = w2.shape[1]
    HC = (HID + P - 1) // P
    HT = HID - (HC - 1) * P
    hrows = [P] * (HC - 1) + [HT]
    STEPS = DEPTH * NB
    XSCALE = float(D) ** -0.5
    YTC = S + 3
    NS = 3
    assert S == 2 * P and D == 2 * P and DEPTH == 2

    xmid = nc.dram_tensor("xmid", [NB, P, T * D], F32, kind="Internal").ap()
    ystream = nc.dram_tensor("ystream", [STEPS, P, T * D], F32, kind="Internal").ap()

    st = ExitStack()
    with st:
        def sb(name, shape, dt=F32):
            return st.enter_context(nc.sbuf_tensor(name, shape, dt))

        def sem(name):
            return st.enter_context(nc.semaphore(name))

        wqkv_hl = [sb(f"wqkv_{n}", [P, KC, 3 * INNER], F32R) for n in ("hi", "lo")]
        wo_hl = [sb(f"wo_{n}", [P, PAIRS, D], F32R) for n in ("hi", "lo")]
        w1_hl = [sb(f"w1_{n}", [P, KC, 2 * HID], F32R) for n in ("hi", "lo")]
        w2_hl = [sb(f"w2_{n}", [P, HC, D], F32R) for n in ("hi", "lo")]
        ident = sb("ident", [P, P])
        shift = sb("shift", [P, 2 * P])
        wmask = sb("wmask", [P, 3 * P])
        rtab = sb("rtab", [P, T, 2, 2 * DH])
        qks = sb("qks", [P, DEPTH, 2 * DH])
        tc_sb = [sb(f"tc_sb{l}", [P, T, 2, DH]) for l in range(DEPTH)]
        ts_sb = [sb(f"ts_sb{l}", [P, T, 2, DH]) for l in range(DEPTH)]
        bqk = sb("bqk", [P, 2, KC])
        bv_bc = sb("bv_bc", [P, D])
        gam_bc = sb("gam_bc", [P, D])
        bet_bc = sb("bet_bc", [P, D])
        b2_bc = [sb(f"b2_bc{l}", [P, D]) for l in range(DEPTH)]
        lgb = sb("lgb", [P, DEPTH, 2, KC])
        b1_sb = sb("b1_sb", [P, DEPTH, 2, HC])
        g_in = sb("g_in", [P, 2])
        tg = sb("tg", [P, 2])
        nhalf = sb("nhalf", [P, 2 * HEADS])

        XTILES = 17
        arena = sb("arena", [P, XTILES + 3, T * D])
        x_in, c_in, m_raw, x_res, xn, xnT, cT, xqT, xkT, xv, mbias, xs, xp, xpT, xc, x_mid, y_new = (
            arena[:, i, :].rearrange("p (t d) -> p t d", t=T) for i in range(XTILES))
        m_in = m_raw.bitcast(I32)
        wq_sb, wk_sb, wv_sb = (arena[:, XTILES + i, :].rearrange("p (k d) -> p k d", k=KC) for i in range(3))
        x1b, yo, xm_res = (arena[:, XTILES + i, :].rearrange("p (t d) -> p t d", t=T) for i in range(3))
        raw = arena[:, 0:XTILES, :].rearrange("p i n -> p (i n)")
        cols = [0]
        for c in (KC * 3 * INNER, PAIRS * D, KC * 2 * HID, HC * D):
            cols.append(cols[-1] + c)
        assert cols[-1] <= XTILES * T * D
        wqkv_raw, wo_raw, w1_raw, w2_raw = (
            raw[:, cols[i]:cols[i + 1]].rearrange("p (k n) -> p k n", k=k)
            for i, k in enumerate((KC, PAIRS, KC, HC)))
        xst = sb("xst", [P, 3, T, 6])
        xmv = sb("xmv", [P, 3, T, 2])
        xrs = sb("xrs", [P, 3, T])
        xmx, xnb, xl, xrl = (sb(n, [P, T]) for n in ("xmx", "xnb", "xl", "xrl"))

        y_next = sb("y_next", [P, T, D])
        y_res = sb("y_res", [P, T, D])
        yT = [sb(f"yT_{n}", [P, KC * YTC], F32R) for n in ("hi", "lo")]
        turned = sb("turned", [P, 3 * 2 * INNER])
        t1 = turned[:, 0:T * 2 * INNER].rearrange("p (t n) -> p t n", t=T)
        t2 = turned[:, T * 2 * INNER:3 * 2 * INNER]
        sqb = sb("sqb", [P, 2 * INNER])
        ss = sb("ss", [P, T, 2 * HEADS])
        rn = sb("rn", [P, T, 2 * HEADS])
        rn8 = sb("rn8", [P, T, HEADS])
        nrn8 = sb("nrn8", [P, T, HEADS])
        qz = sb("qz", [P, HEADS, S])
        kT = sb("kT", [P, PAIRS, S])
        vz = sb("vz", [P, T, PAIRS, 3, DH])
        sm = sb("sm", [P, NS, 3 * P])
        pr = sb("pr", [P, NS, 3 * P])
        pT = sb("pT", [P, 2, 3 * P])
        mx, nb, ls, rl = (sb(n, [P, HEADS, T]) for n in ("mx", "nb", "ls", "rl"))
        oT = [sb(f"oT_{n}", [P, PAIRS, S], F32R) for n in ("hi", "lo")]
        x1 = sb("x1", [P, T, D])
        hst = sb("hst", [P, T, 2, 6])
        hmv = sb("hmv", [P, T, 2])
        hrs = sb("hrs", [P, T])
        hn = sb("hn", [P, T, D])
        hT = [sb(f"hT_{n}", [P, KC, S], F32R) for n in ("hi", "lo")]
        gl = sb("gl", [P, 2, S])
        u_pair = sb("u_pair", [P, 2, S])
        hn_flat = hn[:].rearrange("p t d -> p (t d)")
        u_full = [u_pair[:, 0, :], u_pair[:, 1, :], hn_flat[:, 0:S], hn_flat[:, S:2 * S]]
        u = [sb(f"u_{n}", [P, HC, S], F32R) for n in ("hi", "lo")]

        ps = st.enter_context(nc.psum_tensor("ps", [P, 8, 512], F32))

        def bank(i):
            return ps[:, i, :]

        def halves(i):
            return ps[:, i, :].rearrange("p (t n) -> p t n", t=2)

        ident_loaded, wx_in, cst_in, rot_in, cst2_in, wa_in, wb_in = (
            sem(n) for n in ("ident_loaded", "wx_in", "cst_in", "rot_in", "cst2_in", "wa_in", "wb_in"))
        w_high, w_ready, w2_ready = sem("w_high"), sem("w_ready"), sem("w2_ready")
        b1_mm, b1_done, w1_scaled = sem("b1_mm"), sem("b1_done"), sem("w1_scaled")
        zeros_set, nhalf_set, tanh_done, prep_done = sem("zeros_set"), sem("nhalf_set"), sem("tanh_done"), sem("prep_done")
        dve_passed, pool_passed = sem("dve_passed"), sem("pool_passed")
        x_loaded, c_loaded, m_loaded, xres_loaded = (
            sem(n) for n in ("x_loaded", "c_loaded", "m_loaded", "xres_loaded"))
        xmid_stored, y_stored = sem("xmid_stored"), sem("y_stored")
        stats, var, eps_add, rstd_done = (
            [sem(f"{n}_{k}") for k in ("x", "ctx", "mid")] for n in ("stats", "var", "eps", "rstd"))
        (xn_done, c_tr, xn_tr, cT_done, xnT_done, k_mm, q_mm, v_mm, kT_x, qT_x,
         v_x, s_mm, mb_done, smax, nbx, exp_x, rlx, p_tr, pT_x, ctx_mm, xc_done, tn_done, tg_done,
         xmid_done, xrb_done, y_done_x) = (sem(n) for n in (
             "xn_done", "c_tr", "xn_tr", "cT_done", "xnT_done", "k_mm", "q_mm",
             "v_mm", "kT_x", "qT_x", "v_x", "s_mm", "mb_done", "smax", "nbx", "exp_x", "rlx", "p_tr",
             "pT_x", "ctx_mm", "xc_done", "tn_done", "tg_done", "xmid_done", "xrb_done", "y_done_x"))
        ynext_in, yres_in, xm_in, res_stored = (
            sem(n) for n in ("ynext_in", "yres_in", "xm_in", "res_stored"))
        (y_tr, sh_mm, yT_high, yT_done, qk_mm, v_mm2, sq_done, ss_done, ssc_done, rn_done, rn8_done, rot_done, sum_done, ksum_done,
         ks_done, v_done, o_high, hT_high, u_raw, u_high, qk_tr, q_done, k_done, s_mm2, mx_done, nb_done, e_done, rl_done,
         pn_done, pt_tr, pT_done, pv_mm, o_done, wo_mm, x1_done, hbn_a, hbn, heps, hrstd, hn_done, h_tr,
         hT_done, up_mm, gl_done, u_done, xb_done, dn_mm, yo_done, res_done) = (sem(n) for n in (
             "y_tr", "sh_mm", "yT_high", "yT_done", "qk_mm", "v_mm2", "sq_done", "ss_done", "ssc_done", "rn_done",
             "rn8_done", "rot_done", "sum_done", "ksum_done", "ks_done", "v_done", "o_high", "hT_high", "u_raw",
             "u_high", "qk_tr", "q_done", "k_done", "s_mm2",
             "mx_done", "nb_done", "e_done", "rl_done", "pn_done", "pt_tr", "pT_done", "pv_mm", "o_done",
             "wo_mm", "x1_done", "hbn_a", "hbn", "heps", "hrstd", "hn_done", "h_tr", "hT_done", "up_mm",
             "gl_done", "u_done", "xb_done", "dn_mm", "yo_done", "res_done"))

        block = st.enter_context(nc.Block())

        def rows(ap):
            return ap.rearrange("(t p) d -> p t d", p=P)

        def flat(t):
            return t[:].rearrange("p t d -> p (t d)")

        def run_x(eng, turn, between=lambda b: None):
            turn(0, True, False, False, True)
            between(1)
            turn(1, True, True, False, True)
            between(2)
            turn(2, True, True, True, True)
            with eng.Fori(3, NB - 1) as b:
                turn(b, True, True, True, True)
            turn(NB - 1, True, True, True, False)
            between(NB)
            turn(NB, False, True, True, False)
            between(NB + 1)
            turn(NB + 1, False, False, True, False)

        FIRST, LAST_W2, PIECES = 4, 6, 8
        VPIECES = FIRST + PIECES - LAST_W2

        def raws(l):
            if l == 0:
                return [turned[:].rearrange("p (k n) -> p k n", k=KC), kT[:], w1_raw, w2_raw]
            return [wqkv_raw, wo_raw, w1_raw, w2_raw]

        def pieces(l, first):
            full = raws(l)
            found = []
            if first:
                for j in range(3):
                    c = slice(j * INNER, (j + 1) * INNER)
                    found.append((full[0][:, :, c], wqkv_hl[0][:, :, c], wqkv_hl[1][:, :, c]))
                found.append((full[1], wo_hl[0][:], wo_hl[1][:]))
            else:
                for c, r in ((slice(0, HC - 1), P), (slice(HC - 1, HC), HT)):
                    found.append((full[3][0:r, c, :], w2_hl[0][0:r, c, :], w2_hl[1][0:r, c, :]))
                for k in range(KC):
                    found.append((full[2][:, k, :], w1_hl[0][:, k, :], w1_hl[1][:, k, :]))
            return found

        def run_steps(eng, step):
            step(0, 0, None)
            step(1, 0, 0)
            with eng.Fori(2, NB) as s:
                step(s, 0, 0)
            step(NB, 1, 0)
            with eng.Fori(NB + 1, STEPS - 1) as s:
                step(s, 1, 1)
            step(STEPS - 1, 1, 1)
            step(STEPS, None, 1)

        @block.sync
        def _(sp):
            def load_x(b):
                sp.dma_start(x_in, rows(x[b])).then_inc(x_loaded, 16)

            def load_c(b):
                sp.dma_start(c_in, rows(ctx_in[b])).then_inc(c_loaded, 16)

            def load_m(b):
                sp.dma_start(m_in, rows(mask[b])).then_inc(m_loaded, 16)

            sp.dma_start(ident[:], ident_in).then_inc(ident_loaded, 16)
            load_c(0)
            load_x(0)
            for w, dst in ((Wk, wk_sb), (Wv, wv_sb), (Wq, wq_sb)):
                sp.dma_start(dst, w.rearrange("(k p) n -> p k n", p=P)).then_inc(wx_in, 16)
            load_m(0)
            small = [(bqk[:, 0, :], bq.rearrange("(m p) -> p m", p=P)),
                     (bqk[:, 1, :], bk.rearrange("(m p) -> p m", p=P)),
                     (bv_bc[:], bv.partition_broadcast(P)),
                     (gam_bc[:], ln_gamma.partition_broadcast(P)),
                     (bet_bc[:], ln_beta.partition_broadcast(P)),
                     (g_in[:, 0:1], g_xattn.partition_broadcast(P)),
                     (g_in[:, 1:2], g_ffn.partition_broadcast(P)),
                     (rtab[:], rot_tab)]
            for l in range(DEPTH):
                small += [(qks[:, l, 0:DH], q_scale[l, :].partition_broadcast(P)),
                          (qks[:, l, DH:2 * DH], k_scale[l, :].partition_broadcast(P))]
            small += [(shift[:], shift_in), (wmask[:], win_mask)]
            for l in range(DEPTH):
                small += [(b2_bc[l][:], b2[l, :].partition_broadcast(P)),
                          (lgb[:, l, 0, :], ln_g[l, :].rearrange("(k p) -> p k", p=P)),
                          (lgb[:, l, 1, :], ln_b[l, :].rearrange("(k p) -> p k", p=P))]
                for half in range(2):
                    o = half * HID
                    small += [(b1_sb[:, l, half, 0:HC - 1],
                               b1[l, o:o + HID - HT].rearrange("(c p) -> p c", p=P)),
                              (b1_sb[0:HT, l, half, HC - 1:HC],
                               b1[l, o + HID - HT:o + HID].unsqueeze(1))]
            assert 16 * len(small[12:]) == CONSTS
            for dst, src in small[:7]:
                sp.dma_start(dst, src, allow_slow_non_contiguous=True).then_inc(cst_in, 16)

            def load_layer(l, part):
                wqkv_to, wo_to, w1_to, w2_to = raws(l)
                if part == 0:
                    sp.dma_start(wqkv_to, wqkv[l].rearrange("(k p) n -> p k n", p=P)).then_inc(wa_in, 16)
                elif part == 1:
                    sp.dma_start(wo_to, wo[l].rearrange("(k p) n -> p k n", p=P)).then_inc(wa_in, 16)
                else:
                    sp.dma_start(w1_to, w1[l].rearrange("(k p) n -> p k n", p=P)).then_inc(wb_in, 16)
                    sp.dma_start(w2_to[:, 0:HC - 1, :],
                                 w2[l, 0:HID - HT, :].rearrange("(c p) n -> p c n", p=P)).then_inc(wb_in, 16)
                    sp.dma_start(w2_to[0:HT, HC - 1, :], w2[l, HID - HT:HID, :]).then_inc(wb_in, 16)

            def load_constants(which):
                for dst, src in which:
                    sp.dma_start(dst, src, allow_slow_non_contiguous=True).then_inc(cst2_in, 16)

            def turn(b, project, weigh, finish, ahead):
                if isinstance(b, int) and b == NB + 1:
                    load_constants(small[12:][12:])
                if ahead:
                    sp.wait_ge(xn_done, T * (b + 1))
                    load_x(b + 1)
                if isinstance(b, int) and b == NB - 1:
                    first_input()
                if finish:
                    wait(sp, xmid_done, b - 2)
                    sp.dma_start(x_res, rows(x[b - 2])).then_inc(xres_loaded, 16)
                if ahead:
                    sp.wait_ge(c_tr, b + 1)
                    load_c(b + 1)
                if finish:
                    sp.wait_ge(xmid_done, b - 1)
                    sp.dma_start(xmid[b - 2], arena[:, 15, :]).then_inc(xmid_stored, 16)
                    sp.wait_ge(y_done_x, T * (b - 1))
                    sp.dma_start(ystream[b - 2], arena[:, 16, :]).then_inc(y_stored, 16)
                if ahead:
                    sp.wait_ge(mb_done, b + 1)
                    load_m(b + 1)
                if isinstance(b, int) and b < 2:
                    load_layer(0, b)
                if isinstance(b, int) and b == 1:
                    for dst, src in small[7:12]:
                        sp.dma_start(dst, src, allow_slow_non_contiguous=True).then_inc(rot_in, 16)
                if isinstance(b, int) and NB - 1 <= b <= NB:
                    n = 6 * (b - NB + 1)
                    load_constants(small[12:][n:n + 6])

            def first_input():
                sp.wait_ge(y_stored, 16)
                sp.dma_start(flat(y_next), ystream[0]).then_inc(ynext_in, 16)

            run_x(sp, turn)

            sp.wait_ge(y_stored, 16 * NB)
            sp.wait_ge(xmid_stored, 16 * NB)

            def step(s, la, lf):
                f = s - 1
                if isinstance(s, int) and s == 0:
                    load_layer(0, 2)
                if isinstance(s, int) and s == 1:
                    sp.wait_ge(w_ready, VPIECES)
                    sp.wait_ge(w2_ready, 2)
                    for part in range(3):
                        load_layer(1, part)
                if la is not None:
                    wait(sp, x1_done, s)
                    sp.dma_start(flat(y_res), ystream[s]).then_inc(yres_in, 16)
                    if not (isinstance(s, int) and s == STEPS - 1):
                        wait(sp, y_tr, s + 1)
                        if la == 0:
                            wait(sp, res_stored, 16 * f)
                        else:
                            sp.wait_ge(res_stored, 16 * (s + 2 - NB))
                        sp.dma_start(flat(y_next), ystream[s + 1]).then_inc(ynext_in, 16)
                if lf == 1:
                    sp.wait_ge(res_done, f)
                    sp.dma_start(arena[:, XTILES + 2, :], xmid[f - NB]).then_inc(xm_in, 16)
                if lf is not None:
                    sp.wait_ge(res_done, s)
                    sp.dma_start(rows(out[f - NB]) if lf else ystream[f + NB].rearrange("p (t d) -> p t d", t=T),
                                 yo).then_inc(res_stored, 16)

            run_steps(sp, step)
            sp.wait_ge(res_stored, 16 * STEPS)

        @block.tensor
        def _(pe):
            mm = nc.tensor.matmul

            def transpose_rows(src, b):
                for k in range(KC):
                    for t in range(T):
                        last = nc.tensor.transpose(bank(b)[:, k * S + t * P:k * S + t * P + P],
                                                   src[:, t, k * P:(k + 1) * P], ident[:])
                return last

            def split_product(out, lhsT, rhs, start, stop):
                for i, (a, b) in enumerate(((0, 0), (0, 1), (1, 0))):
                    last = mm(out, lhsT(a), rhs(b), start=(start and i == 0), stop=(stop and i == 2))
                return last

            pe.wait_ge(ident_loaded, 16)

            def project_T(w, src, b, done):
                for m in range(KC):
                    for k in range(KC):
                        last = mm(bank(b)[:, m * S:(m + 1) * S], w[:, k, m * P:(m + 1) * P],
                                  src[:, k, :], start=(k == 0), stop=(k == KC - 1))
                last.then_inc(done, 1)

            def score(b):
                pe.wait_ge(kT_x, KC * (b + 1))
                pe.wait_ge(qT_x, KC * (b + 1))
                wait(pe, smax, T * b)
                for qt in range(T):
                    for k in range(KC):
                        last = mm(bank(5)[:, qt * S:(qt + 1) * S], xqT[:, k, qt * P:(qt + 1) * P],
                                  xkT[:, k, :], start=(k == 0), stop=(k == KC - 1))
                last.then_inc(s_mm, 1)

            def transpose_probs(b):
                pe.wait_ge(exp_x, T * (b + 1))
                wait(pe, pT_x, b)
                for kt in range(T):
                    for qt in range(T):
                        last = nc.tensor.transpose(bank(6)[:, kt * S + qt * P:kt * S + qt * P + P],
                                                   xp[:, qt, kt * P:(kt + 1) * P], ident[:])
                last.then_inc(p_tr, 1)

            def weigh_values(b):
                pe.wait_ge(pT_x, b + 1)
                pe.wait_ge(v_x, b + 1)
                wait(pe, xc_done, T * b)
                for qt in range(T):
                    for kt in range(T):
                        last = mm(bank(7)[:, qt * D:(qt + 1) * D], xpT[:, kt, qt * P:(qt + 1) * P],
                                  xv[:, kt, :], start=(kt == 0), stop=(kt == T - 1))
                last.then_inc(ctx_mm, 1)

            def turn(b, project, weigh, finish, ahead):
                if not project:
                    return
                if project:
                    pe.wait_ge(c_loaded, 16 * (b + 1))
                    wait(pe, cT_done, b)
                    transpose_rows(c_in, 0).then_inc(c_tr, 1)
                    pe.wait_ge(xn_done, T * (b + 1))
                    wait(pe, xnT_done, b)
                    transpose_rows(xn, 1).then_inc(xn_tr, 1)
                if weigh:
                    score(b - 1)
                if project:
                    if isinstance(b, int) and b == 0:
                        pe.wait_ge(wx_in, 48)
                    pe.wait_ge(cT_done, b + 1)
                    wait(pe, kT_x, KC * b)
                    project_T(wk_sb, cT, 2, k_mm)
                    wait(pe, v_x, b)
                    for t in range(T):
                        for k in range(KC):
                            last = mm(bank(4)[:, t * D:(t + 1) * D], cT[:, k, t * P:(t + 1) * P],
                                      wv_sb[:, k, :], start=(k == 0), stop=(k == KC - 1))
                    last.then_inc(v_mm, 1)
                if weigh:
                    transpose_probs(b - 1)
                if project:
                    pe.wait_ge(xnT_done, b + 1)
                    wait(pe, qT_x, KC * b)
                    project_T(wq_sb, xnT, 3, q_mm)
                if weigh:
                    weigh_values(b - 1)

            run_x(pe, turn)

            pe.wait_ge(zeros_set, ZEROS)
            pe.wait_ge(ynext_in, 16)
            pe.wait_ge(cT_done, NB)
            transpose_rows(y_next, 0).then_inc(y_tr, 1)

            def bias_products(l):
                pe.wait_ge(wb_in, 48 * (l + 1))
                pe.wait_ge(mx_done, T * (HEADS * NB * l + HEADS - 2))
                for c in range(HC):
                    for half in range(2):
                        o = half * HID + c * P
                        for k in range(KC):
                            last = mm(ps[0:hrows[c], 2, half * HC + c:half * HC + c + 1],
                                      w1_raw[:, k, o:o + hrows[c]], lgb[:, l, 1, k:k + 1],
                                      start=(k == 0), stop=(k == KC - 1))
                last.then_inc(b1_mm, 1)

            def step(s, la, lf):
                f = s - 1

                def project(t, parts):
                    i = 0 if t == 0 else 3
                    if t == 0 and 0 in parts:
                        pe.wait_ge(yT_done, s + 1)
                        if isinstance(s, int) and s == 0:
                            pe.wait_ge(xnT_done, NB)
                            pe.wait_ge(kT_x, KC * NB)
                            pe.wait_ge(qT_x, KC * NB)
                            pe.wait_ge(v_x, NB)
                    elif 0 in parts:
                        wait(pe, pT_done, HEADS * s)
                    for j in parts:
                        if j == 2:
                            if t == 0:
                                wait(pe, x1_done, s)
                            else:
                                pe.wait_ge(v_done, T * s + t)
                        if t == 0 and isinstance(s, int) and s in (0, NB):
                            pe.wait_ge(w_ready, VPIECES * la + j + 1)
                        o = bank(i + j) if j < 2 else bank(2)
                        for k in range(KC):
                            c0 = k * YTC - k + t * P
                            last = split_product(o, lambda a: yT[a][:, c0:c0 + P],
                                                 lambda a: wqkv_hl[a][:, k, j * INNER:(j + 1) * INNER],
                                                 k == 0, k == KC - 1)
                        last.then_inc((qk_mm, qk_mm, v_mm2)[j], 1)

                def up(c):
                    i, r = 5 + c % 2, hrows[c]
                    if c == 0:
                        pe.wait_ge(hT_done, s)
                        if lf == 1 or (isinstance(s, int) and s == 1):
                            pe.wait_ge(w_ready, VPIECES * (lf + 1))
                            pe.wait_ge(w2_ready, 2 * (lf + 1))
                    if c < 2:
                        pe.wait_ge(o_done, PAIRS * s)
                    else:
                        pe.wait_ge(u_raw, HC * f + c - 1)
                    for half in range(2):
                        o = half * HID + c * P
                        for k in range(KC):
                            last = split_product(ps[0:r, i, half * S:(half + 1) * S],
                                                 lambda a: w1_hl[a][:, k, o:o + r], lambda a: hT[a][:, k, :],
                                                 k == 0, k == KC - 1)
                    last.then_inc(up_mm, 1)

                def tr_heads(t, j):
                    i = 0 if t == 0 else 3
                    if j == 0:
                        pe.wait_ge(sq_done, 2 * (T * s + t + 1))
                    pe.wait_ge((sum_done, ks_done)[j], T * s + t + 1)
                    for c in range(PAIRS):
                        last = nc.tensor.transpose(bank(i + j)[:, c * P:(c + 1) * P],
                                                   t1[:, t, j * INNER + c * P:j * INNER + (c + 1) * P],
                                                   ident[:])
                    last.then_inc(qk_tr, 1)

                def scores_own(h):
                    if h >= NS:
                        pe.wait_ge(mx_done, T * (HEADS * s + h - NS + 1))
                    mm(bank(h % NS)[:, 0:P], qz[:, h, 0:P], kT[:, h // 2, 0:P], start=True, stop=True)

                def scores_both(h):
                    mm(bank(h % NS)[:, P:3 * P], qz[:, h, P:S], kT[:, h // 2, :], start=True, stop=True)\
                        .then_inc(s_mm2, 1)

                def tr_probs(h):
                    b, p = bank(3 + h % 2), pr[:, h % NS, :]
                    pe.wait_ge(pn_done, T * (HEADS * s + h + 1))
                    if h >= 2:
                        pe.wait_ge(pT_done, HEADS * s + h - 1)
                    nc.tensor.transpose(b[:, 0:P], p[:, 2 * P:3 * P], ident[:])
                    nc.tensor.transpose(b[:, P:2 * P], p[:, 0:P], ident[:])
                    nc.tensor.transpose(b[:, 2 * P:3 * P], p[:, P:2 * P], ident[:]).then_inc(pt_tr, 1)

                def weighted(h):
                    pair, j = h // 2, h % 2
                    b = bank(5 + pair % 2)
                    pe.wait_ge(pT_done, HEADS * s + h + 1)
                    if j == 0:
                        if pair < 2:
                            if lf is not None:
                                pe.wait_ge(u_done, HC * s)
                        else:
                            pe.wait_ge(o_done, PAIRS * s + pair - 1)
                    v = [vz[:, t, pair, j:j + 2, :].rearrange("p a d -> p (a d)") for t in range(T)]
                    mm(b[:, 0:S], v[0], pT[:, h % 2, P:3 * P], start=(j == 0), stop=False)
                    mm(b[:, P:S], v[1], pT[:, h % 2, 0:P], start=False, stop=(j == 1)).then_inc(pv_mm, 1)

                def down(n):
                    t, c = n // HC, n % HC
                    if t == 0:
                        pe.wait_ge(u_done, HC * f + c + 1)
                    last = split_product(bank(7)[:, t * D:(t + 1) * D], lambda a: u[a][:, c, t * P:(t + 1) * P],
                                         lambda a: w2_hl[a][:, c, :], c == 0, c == HC - 1)
                    if n == T * HC - 1:
                        last.then_inc(dn_mm, 1)

                def shift_rows():
                    pe.wait_ge(x1_done, s)
                    wait(pe, res_done, f)
                    o = bank(7)[:, 0:T * P].rearrange("p (t n) -> p t n", t=T)
                    mm(o[:, 0, :], shift[:, 0:P], x1[:, 0, P:D], start=True, stop=True)
                    mm(o[:, 1, :], shift[:, 0:P], x1[:, 1, P:D], start=True, stop=False)
                    mm(o[:, 1, :], shift[:, P:2 * P], x1[:, 0, P:D], start=False, stop=True).then_inc(sh_mm, 1)

                A, F = la is not None, lf is not None
                first = isinstance(s, int) and s == 0
                if first:
                    score(NB - 1)
                if A:
                    project(0, (0,))
                if F:
                    shift_rows()
                if A:
                    project(0, (1,))
                if first:
                    transpose_probs(NB - 1)
                if A:
                    project(0, (2,))
                if first:
                    weigh_values(NB - 1)
                if A:
                    project(1, (0,))
                if F:
                    pe.wait_ge(hn_done, s)
                    transpose_rows(hn, 7).then_inc(h_tr, 1)
                if A:
                    project(1, (1, 2))
                if F:
                    up(0)
                    up(1)
                if A:
                    tr_heads(0, 0)
                if F:
                    up(2)
                if A:
                    tr_heads(0, 1)
                if F:
                    for c in range(3, HC):
                        up(c)
                if A:
                    tr_heads(1, 0)
                    tr_heads(1, 1)
                if A:
                    pe.wait_ge(q_done, 2 * T * s + 2)
                    pe.wait_ge(k_done, T * s + 1)
                    pe.wait_ge(v_done, T * (s + 1))
                    for h in range(NS):
                        scores_own(h)
                    pe.wait_ge(q_done, 2 * T * (s + 1))
                    pe.wait_ge(k_done, T * (s + 1))
                    for h in range(NS):
                        scores_both(h)
                n = 0
                if A and F:
                    for n in range(HC - 1):
                        down(n)
                    n = HC - 1
                if A:
                    for h in range(HEADS + 1):
                        if h + NS < HEADS:
                            scores_own(h + NS)
                            scores_both(h + NS)
                        if h < HEADS:
                            tr_probs(h)
                        if isinstance(s, int) and s in (0, NB) and h == HEADS - 1:
                            bias_products(la)
                        if F:
                            while (n - HC + 1) * HEADS < (T * HC - 2 - HC + 1) * h:
                                down(n)
                                n += 1
                        if h:
                            weighted(h - 1)
                    if not (isinstance(s, int) and s == STEPS - 1):
                        pe.wait_ge(ynext_in, 16 * (s + 2))
                        pe.wait_ge(mx_done, T * HEADS * (s + 1))
                        transpose_rows(y_next, 0).then_inc(y_tr, 1)
                if F:
                    while n < T * HC:
                        down(n)
                        n += 1
                if A:
                    pe.wait_ge(o_done, PAIRS * (s + 1))
                    if isinstance(s, int) and s in (0, NB):
                        pe.wait_ge(w_ready, VPIECES * la + FIRST)
                        pe.wait_ge(b1_done, 2 * (la + 1))
                    for t in range(T):
                        for c in range(PAIRS):
                            last = split_product(bank(2)[:, t * D:(t + 1) * D],
                                                 lambda a: oT[a][:, c, t * P:(t + 1) * P],
                                                 lambda a: wo_hl[a][:, c, :], c == 0, c == PAIRS - 1)
                    last.then_inc(wo_mm, 1)

            run_steps(pe, step)

        @block.scalar
        def _(act):
            A = nc.scalar.activation

            def high_parts(l, first, which=slice(None)):
                act.wait_ge(wa_in if first else wb_in, 16 * (2 if first else 3) * (l + 1))
                if l:
                    act.wait_ge(wo_mm if first else dn_mm, NB)
                for i, (full, high, low) in list(enumerate(pieces(l, first)))[which]:
                    if not first and i >= LAST_W2 - FIRST:
                        act.wait_ge(w1_scaled, KC * l + i + 1 - (LAST_W2 - FIRST))
                    A(high, full, ACT.Copy).then_inc(w_high, 1)

            def turn(b, project, weigh, finish, ahead):
                def projected(i):
                    mm_done, done, dst, j = ((k_mm, kT_x, xkT, 1), (q_mm, qT_x, xqT, 0))[i]
                    act.wait_ge(mm_done, b + 1)
                    wait(act, s_mm, b)
                    if isinstance(b, int) and b == 0:
                        act.wait_ge(cst_in, 16 * 7)
                    for m in range(KC):
                        A(dst[:, m, :], halves(2 + i)[:, m, :], ACT.Identity,
                          bias=bqk[:, j, m:m + 1]).then_inc(done, 1)

                if project:
                    act.wait_ge(c_tr, b + 1)
                    wait(act, v_mm, b)
                    A(cT, halves(0), ACT.Copy).then_inc(cT_done, 1)
                    act.wait_ge(xn_tr, b + 1)
                    wait(act, q_mm, b)
                    A(xnT, halves(1), ACT.Copy).then_inc(xnT_done, 1)
                last_projection = isinstance(b, int) and b == NB - 1
                if last_projection:
                    high_parts(0, True, slice(0, 2))
                if weigh:
                    act.wait_ge(nbx, b)
                    wait(act, rlx, b - 1)
                    wait(act, p_tr, b - 1)
                    for t in range(T):
                        A(xp[:, t, :], xs[:, t, :], ACT.Exp, bias=xnb[:, t:t + 1], scale=XSCALE,
                          accum_out=xl[:, t:t + 1]).then_inc(exp_x, 1)
                if project:
                    projected(0)
                if weigh:
                    act.wait_ge(p_tr, b)
                    wait(act, ctx_mm, b - 1)
                    A(xpT, halves(6), ACT.Copy).then_inc(pT_x, 1)
                if last_projection:
                    high_parts(0, True, slice(2, 3))
                if project:
                    projected(1)
                if last_projection:
                    high_parts(0, True, slice(3, 4))

            def evac_yT(n):
                act.wait_ge(y_tr, n)
                dst = yT[0][:].rearrange("p (k c) -> p k c", c=YTC)[:, :, 0:S]
                A(dst, halves(0), ACT.Copy).then_inc(yT_high, 1)

            def between(b):
                if b == 1:
                    A(tg[:], g_in[:], ACT.Tanh).then_inc(tanh_done, 1)
                if b == NB:
                    act.wait_ge(zeros_set, ZEROS)
                    evac_yT(1)

            run_x(act, turn, between)

            def step(s, la, lf):
                f = s - 1

                def squares(t, j):
                    act.wait_ge(qk_mm, 2 * (T * s + t) + j + 1)
                    wait(act, ss_done, 2 * (T * s + t) + j - 1)
                    i = 0 if t == 0 else 3
                    A(sqb[:, j * INNER:(j + 1) * INNER], bank(i + j), ACT.Square).then_inc(sq_done, 1)

                def values(t):
                    act.wait_ge(v_mm2, T * s + t + 1)
                    wait(act, pv_mm, HEADS * s)
                    A(vz[:, t, :, 0:3:2, :], bank(2).rearrange("p (a j d) -> p a j d", a=PAIRS, j=2),
                      ACT.Copy).then_inc(v_done, 1)

                def gelu(c):
                    act.wait_ge(up_mm, HC * f + c + 1)
                    wait(act, u_raw, HC * f + max(0, c - 1))
                    r = hrows[c]
                    A(gl[0:r, c % 2, :], ps[0:r, 5 + c % 2, S:2 * S], ACT.Gelu,
                      bias=b1_sb[0:r, lf, 1, c:c + 1]).then_inc(gl_done, 1)

                def high_u(c):
                    act.wait_ge(u_raw, HC * f + c + 1)
                    r = hrows[c]
                    A(u[0][0:r, c, :], u_full[c % 4][0:r, :], ACT.Copy).then_inc(u_high, 1)

                def queries_T(t):
                    i = 0 if t == 0 else 3
                    act.wait_ge(qk_tr, 2 * (T * s + t) + 1)
                    wait(act, s_mm2, HEADS * s)
                    q = qz[:].rearrange("p (c j) n -> p c j n", j=2)
                    for j in range(2):
                        lo = j * DH
                        A(q[lo:lo + DH, :, j, t * P:(t + 1) * P],
                          ps[lo:lo + DH, i, :].rearrange("p (c n) -> p c n", c=PAIRS), ACT.Copy)\
                            .then_inc(q_done, 1)

                def keys_T(t):
                    i = 0 if t == 0 else 3
                    act.wait_ge(qk_tr, 2 * (T * s + t) + 2)
                    A(kT[:, :, t * P:(t + 1) * P], bank(i + 1).rearrange("p (c n) -> p c n", c=PAIRS),
                      ACT.Copy).then_inc(k_done, 1)

                def exps(h):
                    act.wait_ge(nb_done, HEADS * s + h + 1)
                    if h >= NS:
                        act.wait_ge(pt_tr, HEADS * s + h - NS + 1)
                    wait(act, rl_done, HEADS * s)
                    for t, (a, b) in enumerate(((0, P), (P, 3 * P))):
                        A(pr[:, h % NS, a:b], sm[:, h % NS, a:b], ACT.Exp, bias=nb[:, h, t:t + 1],
                          scale=rn8[:, t, h:h + 1], accum_out=ls[:, h, t:t + 1]).then_inc(e_done, 1)

                def probs_T(h):
                    act.wait_ge(pt_tr, HEADS * s + h + 1)
                    wait(act, pv_mm, HEADS * s + h - 1)
                    A(pT[:, h % 2, :], bank(3 + h % 2)[:, 0:3 * P], ACT.Copy).then_inc(pT_done, 1)

                def heads_out(pair):
                    act.wait_ge(pv_mm, HEADS * s + 2 * pair + 2)
                    wait(act, wo_mm, s)
                    A(oT[0][:, pair, :], bank(5 + pair % 2)[:, 0:S], ACT.Copy).then_inc(o_high, 1)

                if isinstance(s, int) and s == NB:
                    high_parts(1, True)
                if la is not None:
                    squares(0, 0)
                    squares(0, 1)
                    values(0)
                if lf is not None:
                    act.wait_ge(h_tr, s)
                    wait(act, up_mm, HC * f)
                    A(hT[0][:], halves(7), ACT.Copy).then_inc(hT_high, 1)
                if la is not None:
                    squares(1, 0)
                    squares(1, 1)
                if lf is not None:
                    gelu(0)
                if la is not None:
                    values(1)
                if lf is not None:
                    gelu(1)
                    high_u(0)
                if la is not None:
                    queries_T(0)
                if lf is not None:
                    gelu(2)
                if la is not None:
                    keys_T(0)
                if lf is not None:
                    high_u(1)
                    gelu(3)
                    high_u(2)
                    gelu(4)
                    high_u(3)
                    gelu(5)
                if la is not None:
                    queries_T(1)
                    keys_T(1)
                if lf is not None:
                    high_u(4)
                if la is not None:
                    exps(0)
                    exps(1)
                    for h in range(HEADS):
                        if h + 2 < HEADS:
                            exps(h + 2)
                        if h >= 3 and h % 2:
                            heads_out((h - 3) // 2)
                        probs_T(h)
                    heads_out(PAIRS - 1)
                    if not (isinstance(s, int) and s == STEPS - 1):
                        evac_yT(s + 2)
                if isinstance(s, int) and s in (0, NB):
                    high_parts(la, False)

            run_steps(act, step)

        @block.vector
        def _(dve):
            V = nc.vector
            V.memset(nhalf[:], -0.5).then_inc(nhalf_set, 1)

            def statistics(kind, n, values):
                for t in range(T):
                    V.bn_stats(xst[:, kind, t, :], values[:, t, :]).then_inc(stats[kind], 1)
                for t in range(T):
                    wait_apart(dve, dve_passed, (stats[kind], T * n + t + 1))
                    V.bn_aggr(xmv[:, kind, t, :], xst[:, kind, t, :]).then_inc(var[kind], 1)

            def normalised(kind, n, dst, src, done):
                dve.wait_ge(rstd_done[kind], n + 1)
                for t in range(T):
                    V.tensor_scalar(dst[:, t, :], src[:, t, :], xmv[:, kind, t, 0:1], xrs[:, kind, t:t + 1],
                                    ALU.subtract, ALU.mult).then_inc(done, 1)

            def context(b):
                dve.wait_ge(ctx_mm, b + 1)
                dve.wait_ge(rlx, b + 1)
                wait(dve, tg_done, b)
                for t in range(T):
                    V.tensor_scalar(xc[:, t, :], halves(7)[:, t, :], xrl[:, t:t + 1], None,
                                    ALU.mult).then_inc(xc_done, 1)
                dve.wait_ge(xc_done, T * (b + 1))
                statistics(1, b, xc)

            def gate_context(b):
                normalised(1, b, xc, xc, tn_done)
                dve.wait_ge(tn_done, T * (b + 1))
                V.tensor_tensor(xc, xc, gam_bc[:].unsqueeze(1).to_broadcast([P, T, D]),
                                ALU.mult).then_inc(tg_done, 1)

            def add_context(b):
                dve.wait_ge(tg_done, b + 1)
                dve.wait_ge(xrb_done, b + 1)
                wait(dve, xmid_stored, 16 * b)
                V.tensor_tensor(x_mid, xc, x_res, ALU.add).then_inc(xmid_done, 1)
                dve.wait_ge(xmid_done, b + 1)
                statistics(2, b, x_mid)

            def normalise_mid(b):
                wait(dve, y_stored, 16 * b)
                normalised(2, b, y_new, x_mid, y_done_x)

            def turn(b, project, weigh, finish, ahead):
                if not weigh and finish:
                    return
                if finish:
                    context(b - 2)
                if weigh:
                    dve.wait_ge(v_mm, b)
                    V.tensor_tensor(xv, halves(4), bv_bc[:].unsqueeze(1).to_broadcast([P, T, D]),
                                    ALU.add).then_inc(v_x, 1)
                if weigh:
                    wait_apart(dve, dve_passed, (s_mm, b), (mb_done, b),
                               (exp_x, T * (b - 1)))
                    for t in range(T):
                        V.tensor_tensor_reduce(xs[:, t, :], halves(5)[:, t, :], mbias[:, t, :], 1.0, NEG,
                                               ALU.add, ALU.max, xmx[:, t:t + 1]).then_inc(smax, 1)
                    dve.wait_ge(smax, T * b)
                    V.tensor_scalar(xnb[:], xmx[:], -XSCALE, None, ALU.mult).then_inc(nbx, 1)
                if finish:
                    gate_context(b - 2)
                if project:
                    dve.wait_ge(m_loaded, 16 * (b + 1))
                    wait(dve, smax, T * b)
                    V.tensor_scalar(mbias, m_in, 0, NEG, ALU.is_equal, ALU.mult).then_inc(mb_done, 1)
                if finish:
                    add_context(b - 2)
                if weigh:
                    dve.wait_ge(exp_x, T * b)
                    wait(dve, xc_done, T * (b - 1))
                    V.reciprocal(xrl[:], xl[:]).then_inc(rlx, 1)
                if ahead:
                    dve.wait_ge(x_loaded, 16 * (b + 2))
                    statistics(0, b + 1, x_in)
                if isinstance(b, int) and b == NB:
                    low_parts(0, True, slice(2, FIRST))
                if finish:
                    normalise_mid(b - 2)
                if ahead:
                    dve.wait_ge(xn_tr, b + 1)
                    normalised(0, b + 1, xn, x_in, xn_done)

            def low_parts(l, first, which=slice(None)):
                for i, (full, high, low) in list(enumerate(pieces(l, first)))[which]:
                    dve.wait_ge(w_high, PIECES * l + (0 if first else FIRST) + i + 1)
                    V.tensor_tensor(low, full, high.bitcast(F32), ALU.subtract).then_inc(w_ready, 1)

            def fold_offset(l):
                dve.wait_ge(b1_mm, l + 1)
                sums = ps[:, 2, 0:2 * HC].rearrange("p (h c) -> p h c", h=2)
                for r, c in ((P, slice(0, HC - 1)), (HT, slice(HC - 1, HC))):
                    V.tensor_tensor(b1_sb[0:r, l, :, c], b1_sb[0:r, l, :, c], sums[0:r, :, c],
                                    ALU.add).then_inc(b1_done, 1)

            def low_yT(n):
                dve.wait_ge(yT_high, n)
                hi, lo = (p[:].rearrange("p (k c) -> p k c", c=YTC)[:, :, 0:S] for p in yT)
                V.tensor_tensor(lo, halves(0), hi.bitcast(F32), ALU.subtract).then_inc(yT_done, 1)

            def between(b):
                if b == 2:
                    dve.wait_ge(tanh_done, 1)
                    V.tensor_scalar(gam_bc[:], gam_bc[:], tg[:, 0:1], None, ALU.mult).then_inc(prep_done, 1)
                    V.tensor_scalar(bet_bc[:], bet_bc[:], tg[:, 0:1], None, ALU.mult).then_inc(prep_done, 1)
                    dve.wait_ge(prep_done, 2)
                if b == NB:
                    low_parts(0, True, slice(0, 2))
                    dve.wait_ge(zeros_set, ZEROS)
                    low_yT(1)

            dve.wait_ge(x_loaded, 16)
            statistics(0, 0, x_in)
            normalised(0, 0, xn, x_in, xn_done)
            dve.wait_ge(cst_in, 16 * 7)
            run_x(dve, turn, between)

            H = DH // 2
            dve.wait_ge(prep_done, 2 + 3 * DEPTH)

            def step(s, la, lf):
                f = s - 1

                def norms(t, j):
                    dve.wait_ge(sq_done, 2 * (T * s + t) + j + 1)
                    wait(dve, rn_done, T * (s - 1) + t + 1 if not isinstance(s, int) or s else 0)
                    V.tensor_reduce(ss[:, t, j * HEADS:(j + 1) * HEADS],
                                    sqb[:, j * INNER:(j + 1) * INNER].rearrange("p (h d) -> p h d", d=DH),
                                    AX.X, ALU.add).then_inc(ss_done, 1)

                def turned_parts(t):
                    i = 0 if t == 0 else 3
                    qk = ps[:, i:i + 2, :].rearrange("p a (h d) -> p a h d", d=DH)
                    return (qk, *(b.rearrange("p (a h d) -> p a h d", a=2, d=DH) for b in (t1[:, t, :], t2)))

                def rotate_cos(t):
                    wait(dve, qk_tr, 2 * (T * (s - 1) + t + 1) if not isinstance(s, int) or s else 0)
                    qk, a1, _ = turned_parts(t)
                    tc = tc_sb[la][:, t].unsqueeze(2).to_broadcast([P, 2, HEADS, DH])
                    V.tensor_tensor(a1, qk, tc, ALU.mult)

                def rotate_sin(t):
                    wait(dve, sum_done, T * s + t)
                    wait(dve, ksum_done, T * s + t)
                    qk, _, a2 = turned_parts(t)
                    ts = ts_sb[la][:, t].unsqueeze(2).to_broadcast([P, 2, HEADS, DH])
                    V.tensor_tensor(a2[:, :, :, 0:H], qk[:, :, :, H:DH], ts[:, :, :, 0:H], ALU.mult)
                    V.tensor_tensor(a2[:, :, :, H:DH], qk[:, :, :, 0:H], ts[:, :, :, H:DH], ALU.mult)\
                        .then_inc(rot_done, 1)

                def add_queries(t):
                    dve.wait_ge(rot_done, T * s + t + 1)
                    V.tensor_tensor(t1[:, t, 0:INNER], t1[:, t, 0:INNER], t2[:, 0:INNER],
                                    ALU.add).then_inc(sum_done, 1)

                def add_keys(t):
                    V.tensor_tensor(t1[:, t, INNER:2 * INNER], t1[:, t, INNER:2 * INNER],
                                    t2[:, INNER:2 * INNER], ALU.add).then_inc(ksum_done, 1)

                def scale_keys(t):
                    dve.wait_ge(ksum_done, T * s + t + 1)
                    dve.wait_ge(rn_done, T * s + t + 1)
                    kh = t1[:, t, INNER:2 * INNER].rearrange("p (h d) -> p h d", d=DH)
                    rk = rn[:, t, HEADS:2 * HEADS].unsqueeze(2).to_broadcast([P, HEADS, DH])
                    V.tensor_tensor(kh, kh, rk, ALU.mult).then_inc(ks_done, 1)

                def low_hT():
                    dve.wait_ge(hT_high, s)
                    V.tensor_tensor(hT[1][:], halves(7), hT[0][:].bitcast(F32), ALU.subtract).then_inc(hT_done, 1)

                def gated(c):
                    dve.wait_ge(gl_done, HC * f + c + 1)
                    wait(dve, dn_mm, f)
                    if c >= 4:
                        dve.wait_ge(u_done, HC * f + c - 3)
                    r = hrows[c]
                    V.scalar_tensor_tensor(u_full[c % 4][0:r, :], ps[0:r, 5 + c % 2, 0:S],
                                           b1_sb[0:r, lf, 0, c:c + 1], gl[0:r, c % 2, :],
                                           ALU.add, ALU.mult).then_inc(u_raw, 1)

                def high_last_u():
                    c, r = HC - 1, hrows[HC - 1]
                    dve.wait_ge(u_raw, HC * s)
                    dve.wait_ge(u_high, HC * s - 1)
                    V.tensor_copy(u[0][0:r, c, :], u_full[c % 4][0:r, :]).then_inc(u_high, 1)

                def low_oT(pair):
                    dve.wait_ge(o_high, PAIRS * s + pair + 1)
                    V.tensor_tensor(oT[1][:, pair, :], bank(5 + pair % 2)[:, 0:S],
                                    oT[0][:, pair, :].bitcast(F32), ALU.subtract).then_inc(o_done, 1)

                def row_max(h):
                    wait_apart(dve, dve_passed, (s_mm2, HEADS * s + h + 1),
                               (e_done, T * (HEADS * s + max(0, h - NS + 1))),
                               (nb_done, HEADS * s))
                    for t, (a, b) in enumerate(((0, P), (P, 3 * P))):
                        V.tensor_tensor_reduce(sm[:, h % NS, a:b], bank(h % NS)[:, a:b], wmask[:, a:b], 1.0,
                                               NEG, ALU.add, ALU.max, mx[:, h, t:t + 1]).then_inc(mx_done, 1)
                    dve.wait_ge(mx_done, T * (HEADS * s + h + 1))
                    dve.wait_ge(rn8_done, 2 * T * (s + 1))
                    V.tensor_tensor(nb[:, h, :], mx[:, h, :], nrn8[:, :, h], ALU.mult).then_inc(nb_done, 1)

                def row_sum(h):
                    dve.wait_ge(e_done, T * (HEADS * s + h + 1))
                    wait(dve, pn_done, T * HEADS * s)
                    V.reciprocal(rl[:, h, :], ls[:, h, :]).then_inc(rl_done, 1)

                A, F = la is not None, lf is not None

                def shifted_halves(t):
                    return (x1[:, t, 0:P], bank(7)[:, t * P:(t + 1) * P])

                def row_statistics():
                    dve.wait_ge(sh_mm, s)
                    for t in range(T):
                        for i, half in enumerate(shifted_halves(t)):
                            V.bn_stats(hst[:, t, i, :], half).then_inc(hbn_a, 1)
                    wait(dve, heps, f)
                    for t in range(T):
                        wait_apart(dve, dve_passed, (hbn_a, 2 * (T * f + t + 1)))
                        V.bn_aggr(hmv[:, t, :], hst[:, t, :, :]).then_inc(hbn, 1)

                def normalise_rows():
                    dve.wait_ge(hrstd, s)
                    wait(dve, h_tr, f)
                    for t in range(T):
                        for i, half in enumerate(shifted_halves(t)):
                            last = V.tensor_scalar(hn[:, t, i * P:(i + 1) * P], half, hmv[:, t, 0:1],
                                                   hrs[:, t:t + 1], ALU.subtract, ALU.mult)
                    last.then_inc(hn_done, 1)

                start = isinstance(s, int) and s == 0
                if isinstance(s, int) and s == NB:
                    low_parts(1, True)
                if F:
                    row_statistics()
                if A:
                    norms(0, 0)
                    norms(0, 1)
                if F:
                    normalise_rows()
                if start:
                    dve.wait_ge(w_ready, FIRST)
                if A:
                    rotate_cos(0)
                if F:
                    low_hT()
                if A:
                    rotate_sin(0)
                    add_queries(0)
                if A:
                    norms(1, 0)
                    norms(1, 1)
                if F:
                    gated(0)
                if A:
                    scale_keys(0)
                if F:
                    gated(1)
                if A:
                    rotate_cos(1)
                if F:
                    gated(2)
                if A:
                    rotate_sin(1)
                if F:
                    gated(3)
                if A:
                    add_queries(1)
                    add_keys(1)
                if A:
                    scale_keys(1)
                if start:
                    context(NB - 1)
                    gate_context(NB - 1)
                    add_context(NB - 1)
                if F:
                    gated(4)
                    gated(5)
                    high_last_u()
                if start:
                    dve.wait_ge(cst2_in, CONSTS)
                if A:
                    row_max(0)
                    row_max(1)
                    row_sum(0)
                    row_max(2)
                    if start:
                        normalise_mid(NB - 1)
                    for h in range(HEADS):
                        if h + 1 < HEADS:
                            row_sum(h + 1)
                        if h + NS < HEADS:
                            row_max(h + NS)
                        if h >= 4 and h % 2 == 0:
                            low_oT((h - 4) // 2)
                    low_oT(PAIRS - 2)
                    if isinstance(s, int) and s in (0, NB):
                        fold_offset(la)
                    low_oT(PAIRS - 1)
                    if not (isinstance(s, int) and s == STEPS - 1):
                        low_yT(s + 2)
                if F:
                    dve.wait_ge(dn_mm, s)
                    dve.wait_ge(xb_done, s)
                    wait(dve, res_stored, 16 * f)
                    V.tensor_tensor(yo, halves(7), x1b, ALU.add).then_inc(yo_done if lf else res_done, 1)
                    if lf == 1:
                        dve.wait_ge(yo_done, s - NB)
                        dve.wait_ge(xm_in, 16 * (s - NB))
                        V.scalar_tensor_tensor(yo, yo, tg[:, 1:2], xm_res,
                                               ALU.mult, ALU.add).then_inc(res_done, 1)
                if A:
                    dve.wait_ge(wo_mm, s + 1)
                    dve.wait_ge(yres_in, 16 * (s + 1))
                    wait(dve, hn_done, s)
                    wait(dve, xb_done, s)
                    V.tensor_tensor(x1[:], halves(2), y_res[:], ALU.add).then_inc(x1_done, 1)
                if isinstance(s, int) and s in (0, NB):
                    dve.wait_ge(b1_done, 2 * (la + 1))
                    low_parts(la, False, slice(LAST_W2 - FIRST, None))

            run_steps(dve, step)

        @block.gpsimd
        def _(pool):
            G = nc.gpsimd
            pool.wait_ge(nhalf_set, 1)

            def rstd(var, dst, a, b, after_a):
                G.tensor_scalar(dst, var, LN_EPS, 1.0, ALU.add, ALU.mult).then_inc(a, 1)
                pool.wait_ge(a, after_a)
                G.tensor_tensor(dst, dst, nhalf[:, 0:T], ALU.pow).then_inc(b, 1)

            def rstd_x(kind, n):
                wait_apart(pool, pool_passed, (var[kind], T * (n + 1)))
                rstd(xmv[:, kind, :, 1], xrs[:, kind, :], eps_add[kind], rstd_done[kind], n + 1)

            def context_rstd(b):
                rstd_x(1, b)
                pool.wait_ge(xres_loaded, 16 * (b + 1))
                G.tensor_tensor(x_res, x_res, bet_bc[:].unsqueeze(1).to_broadcast([P, T, D]),
                                ALU.add).then_inc(xrb_done, 1)

            def turn(b, project, weigh, finish, ahead):
                if not weigh and finish:
                    return
                if finish:
                    context_rstd(b - 2)
                    rstd_x(2, b - 2)
                if ahead:
                    rstd_x(0, b + 1)

            def between(b):
                if b == 1:
                    for part in (qz, vz):
                        G.memset(part[:], 0.0).then_inc(zeros_set, 1)
                if b == 2:
                    for part in (*yT, *u):
                        G.memset(part[:].bitcast(F32), 0.0).then_inc(zeros_set, 1)
                    for part in w2_hl:
                        G.memset(part[:, HC - 1, :].bitcast(F32), 0.0).then_inc(zeros_set, 1)
                    pool.wait_ge(prep_done, 2)
                if b == NB:
                    pool.wait_ge(rot_in, 16 * 5)
                    H = DH // 2
                    for l in range(DEPTH):
                        sc = qks[:, l, :].rearrange("p (a d) -> p a d", a=2).unsqueeze(1).to_broadcast([P, T, 2, DH])
                        cos, sin = (rtab[:, :, i, :].rearrange("p t (a d) -> p t a d", a=2) for i in range(2))
                        G.tensor_tensor(tc_sb[l][:], cos, sc, ALU.mult).then_inc(prep_done, 1)
                        G.tensor_tensor(ts_sb[l][:, :, :, 0:H], sin[:, :, :, 0:H], sc[:, :, :, H:DH],
                                        ALU.mult).then_inc(prep_done, 1)
                        G.tensor_tensor(ts_sb[l][:, :, :, H:DH], sin[:, :, :, H:DH], sc[:, :, :, 0:H],
                                        ALU.mult).then_inc(prep_done, 1)

            rstd_x(0, 0)
            run_x(pool, turn, between)

            def step(s, la, lf):
                f = s - 1

                def inverse_norms(t):
                    wait_apart(pool, pool_passed, (ss_done, 2 * (T * s + t + 1)))
                    G.tensor_scalar(ss[:, t, :], ss[:, t, :], L2_EPS2, 1.0, ALU.max, ALU.mult)\
                        .then_inc(ssc_done, 1)
                    pool.wait_ge(ssc_done, T * s + t + 1)
                    wait(pool, e_done, T * HEADS * s)
                    G.tensor_tensor(rn[:, t, :], ss[:, t, :], nhalf[:], ALU.pow).then_inc(rn_done, 1)

                def score_scales(t):
                    wait_apart(pool, pool_passed, (rn_done, T * s + t + 1))
                    G.tensor_scalar(rn8[:, t, :], rn[:, t, 0:HEADS], QK_SCALE, 1.0, ALU.mult, ALU.mult)\
                        .then_inc(rn8_done, 1)
                    G.tensor_scalar(nrn8[:, t, :], rn[:, t, 0:HEADS], -QK_SCALE, 1.0, ALU.mult, ALU.mult)\
                        .then_inc(rn8_done, 1)

                def add_keys(t):
                    pool.wait_ge(rot_done, T * s + t + 1)
                    G.tensor_tensor(t1[:, t, INNER:2 * INNER], t1[:, t, INNER:2 * INNER], t2[:, INNER:2 * INNER],
                                    ALU.add).then_inc(ksum_done, 1)

                def low_u(c):
                    pool.wait_ge(u_high, HC * f + c + 1)
                    r = hrows[c]
                    G.tensor_tensor(u[1][0:r, c, :], u_full[c % 4][0:r, :], u[0][0:r, c, :].bitcast(F32),
                                    ALU.subtract).then_inc(u_done, 1)

                def scale_w1(l):
                    wait_apart(pool, pool_passed, (b1_mm, l + 1))
                    for k in range(KC):
                        G.tensor_scalar(w1_raw[:, k, :], w1_raw[:, k, :], lgb[:, l, 0, k:k + 1], 1.0,
                                        ALU.mult, ALU.mult).then_inc(w1_scaled, 1)

                def low_w2(l):
                    for i, (full, high, low) in enumerate(pieces(l, False)[0:LAST_W2 - FIRST]):
                        pool.wait_ge(w_high, PIECES * l + FIRST + i + 1)
                        G.tensor_tensor(low, full, high.bitcast(F32), ALU.subtract).then_inc(w2_ready, 1)

                def normalise(h):
                    wait_apart(pool, pool_passed, (rl_done, HEADS * s + h + 1))
                    for t, (a, b) in enumerate(((0, P), (P, 3 * P))):
                        G.tensor_scalar(pr[:, h % NS, a:b], pr[:, h % NS, a:b], rl[:, h, t:t + 1], 1.0,
                                        ALU.mult, ALU.mult).then_inc(pn_done, 1)

                if lf is not None:
                    wait_apart(pool, pool_passed, (hbn, T * s),
                                                (hn_done, f))
                    rstd(hmv[:, :, 1], hrs[:], heps, hrstd, s)
                start = isinstance(s, int) and s == 0
                if la is not None:
                    inverse_norms(0)
                    add_keys(0)
                    score_scales(0)
                if la is not None:
                    inverse_norms(1)
                    score_scales(1)
                if start:
                    context_rstd(NB - 1)
                    rstd_x(2, NB - 1)
                if lf is not None:
                    for c in range(HC):
                        if c == HC - 2:
                            pool.wait_ge(x1_done, s)
                            wait(pool, res_done, f)
                            G.tensor_tensor(x1b, x1[:], b2_bc[lf][:].unsqueeze(1).to_broadcast([P, T, D]),
                                            ALU.add).then_inc(xb_done, 1)
                        low_u(c)
                if la is not None:
                    for h in range(HEADS):
                        normalise(h)
                if isinstance(s, int) and s in (0, NB):
                    scale_w1(la)
                    low_w2(la)

            run_steps(pool, step)


CONSTS = 16 * 16
ZEROS = 8


def host_tables(S):
    import numpy as np
    half = np.arange(0, DH, 2, dtype=np.float32)
    inv = (np.float32(1.0) / np.float32(10000.0) ** (half / np.float32(DH))).astype(np.float32)
    t = np.arange(S, dtype=np.float32)
    fr = t[:, None] * inv[None, :]
    base = (half + np.float32(0.4 * DH)) / np.float32(1.4 * DH)
    power = (t - S // 2) / np.float32(64)
    sc = base[None, :].astype(np.float64) ** power[:, None].astype(np.float64)
    cos, sin = np.cos(fr.astype(np.float64)), np.sin(fr.astype(np.float64))

    def both(a, b):
        return np.concatenate([a, b], axis=1)
    tab = np.stack([both(both(cos * sc, cos * sc), both(cos / sc, cos / sc)),
                    both(both(-sin * sc, sin * sc), both(-sin / sc, sin / sc))], axis=1)
    tab = tab.reshape(S // P, P, 2, 2 * DH).transpose(1, 0, 2, 3)
    i, j = np.arange(P)[:, None], np.arange(P)[None, :]
    own, prev = np.where(j <= i, 0.0, NEG), np.where(j >= i, 0.0, NEG)
    return (np.ascontiguousarray(tab, np.float32),
            np.concatenate([own, prev, own], axis=1).astype(np.float32), np.eye(P, dtype=np.float32),
            np.eye(P, 2 * P, 1, dtype=np.float32))


_INS = ['x', 'ctx_1024', 'mask_BxSxS2_ik1', 'g_xattn', 'g_ffn', 'L0_xattn_Wq', 'L0_xattn_bq', 'L0_xattn_Wk',
        'L0_xattn_bk', 'L0_xattn_Wv', 'L0_xattn_bv', 'L0_xattn_ln_gamma', 'L0_xattn_ln_beta', 'L0_ffn_wqkv',
        'L0_ffn_q_scale', 'L0_ffn_k_scale', 'L0_ffn_wo', 'L0_ffn_ln_g', 'L0_ffn_ln_b', 'L0_ffn_w1',
        'L0_ffn_b1', 'L0_ffn_w2', 'L0_ffn_b2']


def kernel(**inputs):
    import numpy as np
    import concourse.bacc as bacc
    from concourse.bass_utils import run_bass_kernel_spmd

    arrays = {n: np.ascontiguousarray(inputs[n]) for n in _INS}
    tab, win, eye, down = host_tables(arrays['x'].shape[1])
    arrays.update(rot_tab=tab, win_mask=win, identity=eye, row_shift=down)
    nc = bacc.Bacc("TRN2", target_bir_lowering=False, num_devices=1)
    args = [nc.dram_tensor(n, a.shape, mybir.dt.from_np(a.dtype), kind="ExternalInput").ap()
            for n, a in arrays.items()]
    out = nc.dram_tensor("out", arrays['x'].shape, F32, kind="ExternalOutput").ap()
    build(nc, *args, out)
    r = run_bass_kernel_spmd(nc, [arrays], core_ids=[0])
    return r.results[0]["out"]
```
